# Optimizing a Trainium2 kernel written in Bass

```python
import numpy as np
import jax
import jax.numpy as jnp

def _softmax(x, axis=-1):
    return jax.nn.softmax(x, axis=axis)

def _gelu(x):
    return jax.nn.gelu(x, approximate=True)

def _silu(x):
    return jax.nn.silu(x)

def _sigmoid(x):
    return jax.nn.sigmoid(x)

def _layernorm(x, axis=-1, eps=1e-05):
    m = jnp.mean(x, axis=axis, keepdims=True)
    v = jnp.var(x, axis=axis, keepdims=True)
    return (x - m) / jnp.sqrt(v + eps)

def _scatter_add(tgt, idx, src, axis=0):
    return tgt.at[idx].add(src)

def _segment_sum(src, seg, n):
    return jax.ops.segment_sum(src, seg, n)
kernel_name = 'mk_conv_seq_d2_conv_nchw256_r4_32205c'

def setup_inputs(seed: int=0):
    np.random.seed(seed)
    _w = jnp.asarray

    def _rec_inputs():
        import jax
        import jax.numpy as jnp
        _gk = jax.random.key(seed)
        x = -0.000125 + 0.9999 * jax.random.normal(jax.random.fold_in(_gk, 1), (8, 64, 32, 32), jnp.float32)
        return x
    x = _rec_inputs()

    def _L0_conv_setup():
        import jax, jax.numpy as jnp
        import numpy as np
        HEADS = 8
        DIM_HEAD = 32
        EPS = 1e-05
        key = jax.random.key(seed)
        ks = jax.random.split(key, 4)
        dim = 64
        hidden = HEADS * DIM_HEAD
        x = jax.random.normal(ks[0], (8, dim, 32, 32), dtype=jnp.float32)
        g = jnp.ones((1, dim, 1, 1), jnp.float32)
        b = jnp.zeros((1, dim, 1, 1), jnp.float32)
        w_qkv = jax.random.normal(ks[1], (3 * hidden, dim), dtype=jnp.float32) * dim ** (-0.5)
        w_out = jax.random.normal(ks[2], (dim, hidden), dtype=jnp.float32) * hidden ** (-0.5)
        b_out = jnp.zeros((dim,), jnp.float32)
        return {'x': x, 'g': g, 'b': b, 'w_qkv': w_qkv, 'w_out': w_out, 'b_out': b_out}
    _L0_conv_all = _L0_conv_setup()
    _L0_conv_in = {k: v for k, v in _L0_conv_all.items() if k in ('g', 'b', 'w_qkv', 'w_out', 'b_out')}
    del _L0_conv_all

    def _L1_conv_setup():
        import jax, jax.numpy as jnp
        import numpy as np
        from jax import lax
        BN_EPS = 1e-05
        key = jax.random.key(seed)
        k1, k2 = jax.random.split(key)
        B, C, H, Wd = (32, 64, 56, 56)
        x = jax.random.normal(k1, (B, C, H, Wd), dtype=jnp.float32)
        W = jax.random.normal(k2, (C, C, 3, 3), dtype=jnp.float32) * 0.05
        gamma = jnp.ones((C,), dtype=jnp.float32)
        beta = jnp.zeros((C,), dtype=jnp.float32)
        return {'x': x, 'W': W, 'gamma': gamma, 'beta': beta}
    _L1_conv_all = _L1_conv_setup()
    _L1_conv_in = {k: v for k, v in _L1_conv_all.items() if k in ('W', 'gamma', 'beta')}
    del _L1_conv_all
    return {'x': x, 'L0_conv_g': _L0_conv_in['g'], 'L0_conv_b': _L0_conv_in['b'], 'L0_conv_w_qkv': _L0_conv_in['w_qkv'], 'L0_conv_w_out': _L0_conv_in['w_out'], 'L0_conv_b_out': _L0_conv_in['b_out'], 'L1_conv_W': _L1_conv_in['W'], 'L1_conv_gamma': _L1_conv_in['gamma'], 'L1_conv_beta': _L1_conv_in['beta']}

def reference(x, L0_conv_g, L0_conv_b, L0_conv_w_qkv, L0_conv_w_out, L0_conv_b_out, L1_conv_W, L1_conv_gamma, L1_conv_beta):
    import jax
    import jax.numpy as jnp

    def _L0_conv_ref(x, g, b, w_qkv, w_out, b_out):
        import jax, jax.numpy as jnp
        import numpy as np
        HEADS = 8
        DIM_HEAD = 32
        EPS = 1e-05
        B, C, H, W = x.shape
        N = H * W
        scale = DIM_HEAD ** (-0.5)
        mean = jnp.mean(x, axis=1, keepdims=True)
        var = jnp.var(x, axis=1, keepdims=True)
        xn = (x - mean) / jnp.sqrt(var + EPS) * g + b
        qkv = jnp.einsum('bchw,oc->bohw', xn, w_qkv)
        qkv = qkv.reshape(B, 3, HEADS, DIM_HEAD, N)
        q, k, v = (qkv[:, 0], qkv[:, 1], qkv[:, 2])
        q = q * scale
        k = jax.nn.softmax(k, axis=-1)
        context = jnp.einsum('bhcn,bhdn->bhcd', k, v)
        out = jnp.einsum('bhcd,bhcn->bhdn', context, q)
        out = out.reshape(B, HEADS * DIM_HEAD, H, W)
        out = jnp.einsum('bchw,oc->bohw', out, w_out) + b_out[None, :, None, None]
        return out + xn

    def _L1_conv_ref(x, W, gamma, beta):
        import jax, jax.numpy as jnp
        import numpy as np
        from jax import lax
        BN_EPS = 1e-05
        s = jnp.sign(x)
        bw = jnp.sign(W)
        y = lax.conv_general_dilated(s, bw, window_strides=(1, 1), padding=((1, 1), (1, 1)), dimension_numbers=('NCHW', 'OIHW', 'NCHW'))
        mean = jnp.mean(y, axis=(0, 2, 3))
        var = jnp.var(y, axis=(0, 2, 3))
        inv = gamma / jnp.sqrt(var + BN_EPS)
        yn = (y - mean[None, :, None, None]) * inv[None, :, None, None] + beta[None, :, None, None]
        return yn + x

    def _gn(v, G=32, eps=1e-05):
        B_, C_, H_, W_ = v.shape
        g = v.reshape(B_, G, C_ // G, H_, W_)
        m = jnp.mean(g, axis=(2, 3, 4), keepdims=True)
        s = jnp.var(g, axis=(2, 3, 4), keepdims=True)
        return ((g - m) / jnp.sqrt(s + eps)).reshape(v.shape)

    def _ln_c(v, eps=1e-06):
        m = jnp.mean(v, axis=1, keepdims=True)
        s = jnp.var(v, axis=1, keepdims=True)
        return (v - m) / jnp.sqrt(s + eps)

    def _ln_t(v, eps=1e-05):
        m = jnp.mean(v, axis=-1, keepdims=True)
        s = jnp.var(v, axis=-1, keepdims=True)
        return (v - m) / jnp.sqrt(s + eps)

    def _to_tokens(v):
        B_, C_, H_, W_ = v.shape
        return v.reshape(B_, C_, H_ * W_).transpose(0, 2, 1)

    def _from_tokens(t, like):
        B_, C_, H_, W_ = like.shape
        return t.transpose(0, 2, 1).reshape(B_, C_, H_, W_)
    x = _L0_conv_ref(x, L0_conv_g, L0_conv_b, L0_conv_w_qkv, L0_conv_w_out, L0_conv_b_out)
    x = _L1_conv_ref(x, L1_conv_W, L1_conv_gamma, L1_conv_beta)
    return x

_drawn_inputs = setup_inputs


def setup_inputs(seed=0):
    import zlib

    import numpy as np

    out = dict(_drawn_inputs(seed))
    spreads = {'L0_conv_g': (1.0, 0.2),
     'L0_conv_b': (0.0, 0.1),
     'L0_conv_b_out': (0.0, 0.1),
     'L1_conv_gamma': (1.0, 0.2),
     'L1_conv_beta': (0.0, 0.1)}
    factors = {}
    for name, (base, spread) in spreads.items():
        noise = np.random.default_rng([zlib.crc32(name.encode()), seed]).standard_normal(out[name].shape)
        drawn = base * np.exp(spread * noise) if base else spread * noise
        out[name] = jnp.asarray(drawn.astype(out[name].dtype))
    for name, factor in factors.items():
        out[name] = (out[name] * factor).astype(out[name].dtype)
    return out
```

```python
import concourse.bass as bass
from concourse import mybir
from contextlib import ExitStack


def attention_then_binary_conv(nc, x, ln_g, ln_b, w_qkv, w_out, b_out, conv_w, bn_gamma, bn_beta, out):
    f32, bf16, f16 = mybir.dt.float32, mybir.dt.bfloat16, mybir.dt.float16
    ALU, ACT, AX = mybir.AluOpType, mybir.ActivationFunctionType, mybir.AxisListType

    B, C, H, W = x.shape
    P = 128
    N = H * W
    HID = w_out.shape[1]
    DH = 32
    HEADS = HID // DH
    NT = HID // P
    HPT = P // DH
    PAIRS = B // 2
    BANK = 512
    HALVES = N // BANK
    CH = N // P
    CPB = CH // HALVES
    TAPS = conv_w.shape[2] * conv_w.shape[3]
    ROWS = H // HALVES
    SCALE = float(DH) ** -0.5
    LN_EPS = BN_EPS = 1e-5
    LAST = B - 1

    x_d = x.rearrange("(q b) c h w -> q (b c) (h w)", b=2)
    out_d = out.rearrange("(q b) c h w -> q (b c) (h w)", b=2)
    w_d = w_qkv.rearrange("(k t p) i -> k p t i", k=3, p=P)

    with ExitStack() as ctx:
        def sb(name, shape, dt=f32):
            return ctx.enter_context(nc.sbuf_tensor(name, shape, dt))

        def sem(name):
            return ctx.enter_context(nc.semaphore(name))

        ident = sb("ident", [P, P])
        ident_bf = sb("ident_bf", [P, P], bf16)
        mean_mat = sb("mean_mat", [P, P])
        center_mat = sb("center_mat", [P, P])
        fold = sb("fold", [P, 2, C])
        unfold = sb("unfold", [P, P])
        eps = sb("eps", [P, 1])
        wk_in = sb("wk_in", [P, NT, 2, C])
        wq_in = sb("wq_in", [P, NT, 2, C])
        wv_in = sb("wv_in", [P, NT, 2, C])
        wo_in = sb("wo_in", [C, HID])
        wc_in = sb("wc_in", [C, C * TAPS])
        vec = sb("vec", [P, 5])
        G_, B_, BO_, GA_, BE_ = range(5)
        wk_hi = sb("wk_hi", [P, NT, P], bf16)
        wk_lo = sb("wk_lo", [P, NT, P], bf16)
        wo_heads = sb("wo_heads", [P, NT, HPT, C])
        u_all = sb("u_all", [P, HEADS, C])
        wc_sign = sb("wc_sign", [C, TAPS, 2, C], bf16)
        wc_t = sb("wc_t", [P, TAPS, P], bf16)

        X = sb("X", [P, PAIRS, N])
        XN = sb("XN", [P, PAIRS, N])
        xc = sb("xc", [P, 2, N])
        sq = sb("sq", [P, 2, N])
        lnv = sb("lnv", [P, 2, N])
        rstd = sb("rstd", [P, 2, N])
        x_hi = sb("x_hi", [P, 2, N], bf16)
        x_lo = sb("x_lo", [P, 2, N], bf16)
        S = sb("S", [P, B, N], bf16)
        XT = sb("XT", [P, B, CH, 2, C], bf16)
        E = sb("E", [P, NT, N])
        et_hi = sb("et_hi", [P, NT, N], bf16)
        et_lo = sb("et_lo", [P, NT, N], bf16)
        negmax = sb("negmax", [P, NT])
        Z = sb("Z", [P, B, NT])
        rz = sb("rz", [P, NT])
        PT = sb("PT", [P, NT, P])
        R = sb("R", [P, NT, C])
        BD = sb("BD", [P, PAIRS, P])
        bd = sb("bd", [P, 2, P])
        SG = sb("SG", [P, 2, H + 2, W + 2], bf16)
        Y = sb("Y", [P, PAIRS, N], f16)
        ST = sb("ST", [P, PAIRS, HALVES, 6])
        MV = sb("MV", [P, 2])
        FS = sb("FS", [P, 3])
        tiny = sb("tiny", [P, 6])
        T4 = sb("T4", [P, 2, N])

        ps = ctx.enter_context(nc.psum_tensor("ps", [P, 8, BANK], f32))

        def banks(a, n=2):
            return ps[:, a:a + n, :].rearrange("p a n -> p (a n)")

        pc = [banks(0), banks(2)]
        pv = banks(4)
        xt_ps = [ps[:, 6, :].bitcast(bf16), ps[:, 7, :].bitcast(bf16)]
        k_ps = [banks(0), banks(2)]
        t_ps = [ps[:, 4, :], ps[:, 5, :]]
        d_ps = ps[:, 6, 0:NT * P]
        r_ps = ps[:, 7, 0:NT * C]
        m_ps = ps[:, 7, 256:256 + P]
        f_ps = [banks(0), banks(2)]
        c_ps = [banks(4), banks(6)]

        two = range(2)
        x_loaded = [sem(f"x_loaded{s}") for s in two]
        wk_loaded, w_loaded, vec_loaded = sem("wk_loaded"), sem("w_loaded"), sem("vec_loaded")
        zeroed, ident_ready, mats_ready = sem("zeroed"), sem("ident_ready"), sem("mats_ready")
        dve_const = sem("dve_const")
        wkt_done, wot_done, ct_done, u_done = sem("wkt_done"), sem("wot_done"), sem("ct_done"), sem("u_done")
        wkh_ready, wkl_ready, heads_ready, u_ready, wct_ready = (
            sem("wkh_ready"), sem("wkl_ready"), sem("heads_ready"), sem("u_ready"), sem("wct_ready"))
        wsign_ready = sem("wsign_ready")
        centered = [sem(f"centered{s}") for s in two]
        xc_ready = [sem(f"xc_ready{s}") for s in two]
        sq_ready = [sem(f"sq_ready{s}") for s in two]
        var_ready = [sem(f"var_ready{s}") for s in two]
        lnv_ready = [sem(f"lnv_ready{s}") for s in two]
        rstd_ready = [sem(f"rstd_ready{s}") for s in two]
        scaled = [sem(f"scaled{s}") for s in two]
        xn_ready = [sem(f"xn_ready{s}") for s in two]
        hi_ready = [sem(f"hi_ready{s}") for s in two]
        lo_ready = [sem(f"lo_ready{s}") for s in two]
        stacked = [sem(f"stacked{s}") for s in two]
        xt_done = [sem(f"xt_done{s}") for s in two]
        xth_ready, xtl_ready = [sem(f"xth_ready{s}") for s in two], [sem(f"xtl_ready{s}") for s in two]
        k_ready = [sem(f"k_ready{t}") for t in two]
        max_ready = [sem(f"max_ready{t}") for t in two]
        exp_ready = [sem(f"exp_ready{t}") for t in two]
        et_done = [sem(f"et_done{h}") for h in two]
        eth_ready = [sem(f"eth_ready{h}") for h in two]
        etl_ready = [sem(f"etl_ready{h}") for h in two]
        d_done = [sem(f"d_done{t}") for t in two]
        pt_ready, r_done, rz_ready, r_ready, m_done, bd_ready = (
            sem("pt_ready"), sem("r_done"), sem("rz_ready"), sem("r_ready"), sem("m_done"), sem("bd_ready"))
        bds_ready = [sem(f"bds_ready{s}") for s in two]
        f_done = [sem(f"f_done{s}") for s in two]
        x1_ready = [sem(f"x1_ready{s}") for s in two]
        sg_ready = [sem(f"sg_ready{s}") for s in two]
        conv_done = [sem(f"conv_done{s}") for s in two]
        y_ready = [sem(f"y_ready{s}") for s in two]
        st_ready = [sem(f"st_ready{s}") for s in two]
        mv_ready, fold_done, bn_step, bn_act, affine_ready = (
            sem("mv_ready"), sem("fold_done"), sem("bn_step"), sem("bn_act"), sem("affine_ready"))
        t4_ready = [sem(f"t4_ready{s}") for s in two]
        o_ready = [sem(f"o_ready{s}") for s in two]
        stored = sem("stored")

        block = ctx.enter_context(nc.Block())

        @block.sync
        def _(sp):
            sp.dma_start(X[:, 0, :], x_d[0]).then_inc(x_loaded[0], 16)
            sp.dma_start(X[:, 1, :], x_d[1]).then_inc(x_loaded[1], 16)
            for s in two:
                sp.wait_ge(x_loaded[s], 16)
                sp.dma_start(X[:, 2 + s, :], x_d[2 + s]).then_inc(x_loaded[s], 16)
            for i in range(PAIRS // 2):
                for s in two:
                    q = i * 2 + s
                    sp.wait_ge(stacked[s], i * 64)
                    sp.wait_ge(hi_ready[s], i + 1)
                    sp.dma_start(S[0:C, q * 2, :], x_hi[0:C, s, :]).then_inc(stacked[s], 16)
                    sp.dma_start(S[C:P, q * 2 + 1, :], x_hi[C:P, s, :]).then_inc(stacked[s], 16)
                    sp.wait_ge(lo_ready[s], i + 1)
                    sp.dma_start(S[C:P, q * 2, :], x_lo[0:C, s, :]).then_inc(stacked[s], 16)
                    sp.dma_start(S[0:C, q * 2 + 1, :], x_lo[C:P, s, :]).then_inc(stacked[s], 16)
            for i in range(PAIRS // 2):
                for s in two:
                    q = i * 2 + s
                    sp.wait_ge(o_ready[s], i + 1)
                    sp.dma_start(out_d[q], XN[:, q, :]).then_inc(stored, 16)
            sp.wait_ge(stored, 16 * PAIRS)

        @block.gpsimd
        def _(pool):
            nc.gpsimd.memset(ident[:], 0.0).then_inc(zeroed, 1)
            pool.wait_ge(zeroed, 1)
            nc.gpsimd.affine_select(out=ident[:], in_=ident[:], compare_op=ALU.not_equal, fill=1.0, base=0,
                                    pattern=[[-1, P]], channel_multiplier=1).then_inc(ident_ready, 1)
            nc.gpsimd.memset(SG[:], 0.0).then_inc(zeroed, 1)
            nc.gpsimd.memset(BD[:], 0.0).then_inc(zeroed, 1)
            nc.gpsimd.memset(wc_t[:], 0.0).then_inc(zeroed, 1)
            nc.gpsimd.memset(wo_heads[:], 0.0).then_inc(zeroed, 1)
            with pool.Fori(0, PAIRS // 2) as i:
                for s in two:
                    pool.wait_ge(hi_ready[s], i + 1)
                    pool.wait_ge(xt_done[s], i)
                    pool.wait_ge(stacked[s], i * 64)
                    nc.gpsimd.tensor_tensor(x_lo[:, s, :], XN[:, i * 2 + s, :], x_hi[:, s, :],
                                            ALU.subtract).then_inc(lo_ready[s], 1)

        @block.scalar
        def _(act):
            for d in two:
                act.dma_start(wk_in[:, :, d, :], w_d[1]).then_inc(wk_loaded, 16)
            for i, v in enumerate((ln_g.rearrange("a c h w -> c (a h w)"), ln_b.rearrange("a c h w -> c (a h w)"),
                                   b_out.unsqueeze(1), bn_gamma.unsqueeze(1), bn_beta.unsqueeze(1))):
                for d in two:
                    act.dma_start(vec[d * C:d * C + C, i:i + 1], v).then_inc(vec_loaded, 16)
            act.dma_start(wo_in[:], w_out).then_inc(w_loaded, 16)
            for d in two:
                act.dma_start(wv_in[:, :, d, :], w_d[2]).then_inc(w_loaded, 16)
                act.dma_start(wq_in[:, :, d, :], w_d[0]).then_inc(w_loaded, 16)
            act.dma_start(wc_in[:], conv_w.rearrange("o i h w -> o (i h w)")).then_inc(w_loaded, 16)

            act.wait_ge(wkt_done, 1)
            nc.scalar.copy(wk_hi[:].rearrange("p t c -> p (t c)"), ps[:, 6, 0:NT * P]).then_inc(wkh_ready, 1)
            act.wait_ge(w_loaded, 96)
            for d in two:
                nc.scalar.activation(wc_sign[:, :, d, :].rearrange("o t i -> o i t"),
                                     wc_in[:].rearrange("o (i t) -> o i t", t=TAPS), ACT.Sign).then_inc(wsign_ready, 1)

            act.wait_ge(dve_const, 1)
            with act.Fori(0, PAIRS // 2) as i:
                for s in two:
                    act.wait_ge(centered[s], i + 1)
                    act.wait_ge(scaled[s], i)
                    nc.scalar.copy(xc[:, s, :], pc[s]).then_inc(xc_ready[s], 1)
                for s in two:
                    act.wait_ge(var_ready[s], i + 1)
                    nc.scalar.activation(lnv[:, s, :], pv, ACT.Ln, bias=eps[:, 0:1]).then_inc(lnv_ready[s], 1)
                    act.wait_ge(lnv_ready[s], i + 1)
                    act.wait_ge(scaled[s], i)
                    nc.scalar.activation(rstd[:, s, :], lnv[:, s, :], ACT.Exp, scale=-0.5).then_inc(rstd_ready[s], 1)
                for s in two:
                    act.wait_ge(xt_done[s], i + 1)
                    nc.scalar.copy(XT[:, bass.ds(i * 4 + s * 2, 2), :, 0, :].rearrange("p b k c -> p k b c"),
                                   xt_ps[0].rearrange("p (k b c) -> p k b c", k=CH, b=2)).then_inc(xth_ready[s], 1)

            def exp(b, t):
                act.wait_ge(max_ready[t], b + 1)
                if not isinstance(b, int) or b:
                    act.wait_ge(et_done[1], b * 2 + t - 1)
                nc.scalar.activation(E[:, t, :], k_ps[t], ACT.Exp, bias=negmax[:, t:t + 1],
                                     accum_out=Z[:, bass.ds(b, 1), t]).then_inc(exp_ready[t], 1)

            def split_hi(b, t):
                for h in two:
                    act.wait_ge(et_done[h], b * 2 + t + 1)
                    act.wait_ge(d_done[t], b)
                    nc.scalar.copy(et_hi[:, t, h * BANK:(h + 1) * BANK], t_ps[h]).then_inc(eth_ready[h], 1)

            def keep_pt(b):
                act.wait_ge(d_done[1], b + 1)
                act.wait_ge(r_done, b)
                nc.scalar.copy(PT[:].rearrange("p t c -> p (t c)"), d_ps).then_inc(pt_ready, 1)

            def act_step(b, first=False, last=False):
                split_hi(b, 0)
                exp(b, 1)
                if not first:
                    keep_pt(b - 1)
                split_hi(b, 1)
                if not last:
                    exp(b + 1, 0)

            exp(0, 0)
            act_step(0, first=True)
            with act.Fori(1, LAST) as b:
                act_step(b)
            act_step(LAST, last=True)
            keep_pt(LAST)

            with act.Fori(0, PAIRS // 2) as i:
                for s in two:
                    act.wait_ge(bd_ready, B)
                    act.wait_ge(f_done[s], i)
                    nc.scalar.copy(bd[:, s, :], BD[:, i * 2 + s, :]).then_inc(bds_ready[s], 1)
                for s in two:
                    act.wait_ge(x1_ready[s], i + 1)
                    act.wait_ge(conv_done[s], i)
                    nc.scalar.activation(SG[:, s, 1:H + 1, 1:W + 1],
                                         X[:, i * 2 + s, :].rearrange("p (h w) -> p h w", h=H),
                                         ACT.Sign).then_inc(sg_ready[s], 1)
                for s in two:
                    act.wait_ge(conv_done[s], i + 1)
                    nc.scalar.copy(Y[:, i * 2 + s, :], c_ps[s]).then_inc(y_ready[s], 1)

            act.wait_ge(bn_step, 2)
            nc.scalar.activation(tiny[:, 1:2], tiny[:, 0:1], ACT.Ln, bias=eps[:, 0:1]).then_inc(bn_act, 1)
            act.wait_ge(bn_act, 1)
            nc.scalar.activation(tiny[:, 2:3], tiny[:, 1:2], ACT.Exp, scale=-0.5).then_inc(bn_act, 1)
            act.wait_ge(affine_ready, 1)
            with act.Fori(0, PAIRS // 2) as i:
                for s in two:
                    act.wait_ge(o_ready[s], i)
                    nc.scalar.activation(T4[:, s, :], Y[:, i * 2 + s, :], ACT.Identity, bias=tiny[:, 5:6],
                                         scale=tiny[:, 3:4]).then_inc(t4_ready[s], 1)

        @block.vector
        def _(dve):
            nc.vector.memset(mean_mat[:], 0.0).then_inc(mats_ready, 1)
            nc.vector.memset(eps[:], LN_EPS).then_inc(dve_const, 1)
            dve.wait_ge(mats_ready, 1)
            for d in two:
                nc.vector.memset(mean_mat[d * C:d * C + C, d * C:d * C + C], 1.0 / C).then_inc(mats_ready, 1)
            dve.wait_ge(ident_ready, 1)
            dve.wait_ge(mats_ready, 3)
            nc.vector.tensor_tensor(center_mat[:], ident[:], mean_mat[:], ALU.subtract).then_inc(mats_ready, 1)
            nc.vector.tensor_copy(ident_bf[:], ident[:]).then_inc(dve_const, 1)
            nc.vector.tensor_tensor(unfold[:, 0:C], ident[:, 0:C], ident[:, C:P], ALU.add).then_inc(dve_const, 1)
            dve.wait_ge(dve_const, 3)
            for d in two:
                nc.vector.tensor_scalar(fold[:, d, :], unfold[:, 0:C], 0.5, None, ALU.mult).then_inc(dve_const, 1)
            dve.wait_ge(dve_const, 5)
            nc.vector.tensor_tensor(unfold[:], ident[:], fold[:].rearrange("p d c -> p (d c)"),
                                    ALU.subtract).then_inc(dve_const, 1)
            dve.wait_ge(wkh_ready, 1)
            nc.vector.tensor_tensor(wk_lo[:].rearrange("p t c -> p (t c)"), ps[:, 6, 0:NT * P],
                                    wk_hi[:].rearrange("p t c -> p (t c)"), ALU.subtract).then_inc(wkl_ready, 1)
            dve.wait_ge(wot_done, 1)
            dve.wait_ge(zeroed, 5)
            for t in range(NT):
                for h in range(HPT):
                    nc.vector.tensor_copy(wo_heads[h * DH:(h + 1) * DH, t, h, :],
                                          ps[h * DH:(h + 1) * DH, 7, t * C:(t + 1) * C]).then_inc(heads_ready, 1)
            dve.wait_ge(ct_done, 1)
            for d in two:
                nc.vector.tensor_copy(wc_t[d * C:d * C + C, :, d * C:d * C + C],
                                      xt_ps[0][d * C:d * C + C, 0:TAPS * C].rearrange("p (t c) -> p t c", c=C)
                                      ).then_inc(wct_ready, 1)
            dve.wait_ge(u_done, 1)
            nc.vector.tensor_copy(u_all[:].rearrange("p h c -> p (h c)"), ps[:, 7, :]).then_inc(u_ready, 1)

            dve.wait_ge(vec_loaded, 160)
            with dve.Fori(0, PAIRS // 2) as i:
                for s in two:
                    dve.wait_ge(xc_ready[s], i + 1)
                    dve.wait_ge(var_ready[s], i)
                    nc.vector.tensor_tensor(sq[:, s, :], xc[:, s, :], xc[:, s, :], ALU.mult).then_inc(sq_ready[s], 1)
                for s in two:
                    q = i * 2 + s
                    dve.wait_ge(rstd_ready[s], i + 1)
                    nc.vector.scalar_tensor_tensor(XN[:, q, :], xc[:, s, :], vec[:, G_:G_ + 1], rstd[:, s, :],
                                                   op0=ALU.mult, op1=ALU.mult).then_inc(scaled[s], 1)
                    dve.wait_ge(scaled[s], i + 1)
                    nc.vector.tensor_scalar(XN[:, q, :], XN[:, q, :], vec[:, B_:B_ + 1], None,
                                            ALU.add).then_inc(xn_ready[s], 1)
                    dve.wait_ge(xn_ready[s], i + 1)
                    dve.wait_ge(xt_done[s], i)
                    dve.wait_ge(stacked[s], i * 64)
                    dve.wait_ge(lo_ready[s], i)
                    nc.vector.tensor_scalar(x_hi[:, s, :], XN[:, q, :], 1.0, None, ALU.mult).then_inc(hi_ready[s], 1)
                for s in two:
                    dve.wait_ge(xt_done[s], i + 1)
                    nc.vector.tensor_scalar(XT[:, bass.ds(i * 4 + s * 2, 2), :, 1, :].rearrange("p b k c -> p k b c"),
                                            xt_ps[1].rearrange("p (k b c) -> p k b c", k=CH, b=2), 1.0, None,
                                            ALU.mult).then_inc(xtl_ready[s], 1)

            def row_max(b, t):
                dve.wait_ge(k_ready[t], b + 1)
                nc.vector.tensor_reduce(negmax[:, t:t + 1], k_ps[t], AX.X, ALU.max, negate=True
                                        ).then_inc(max_ready[t], 1)

            def split_lo(b, t):
                for h in two:
                    dve.wait_ge(eth_ready[h], b * 2 + t + 1)
                    dve.wait_ge(d_done[t], b)
                    nc.vector.tensor_tensor(et_lo[:, t, h * BANK:(h + 1) * BANK], t_ps[h],
                                            et_hi[:, t, h * BANK:(h + 1) * BANK], ALU.subtract
                                            ).then_inc(etl_ready[h], 1)

            def divide_r(b):
                dve.wait_ge(exp_ready[1], b + 1)
                dve.wait_ge(exp_ready[0], b + 1)
                nc.vector.reciprocal(rz[:], Z[:, bass.ds(b, 1), :].rearrange("p b t -> p (b t)")).then_inc(rz_ready, 1)
                dve.wait_ge(rz_ready, b + 1)
                dve.wait_ge(r_done, b + 1)
                dve.wait_ge(m_done, b)
                for t in range(NT):
                    nc.vector.tensor_scalar(R[:, t, :], r_ps[:, t * C:(t + 1) * C], rz[:, t:t + 1], SCALE,
                                            ALU.mult, ALU.mult).then_inc(r_ready, 1)

            def keep_m(b, q, half):
                lo, hi = half * C, half * C + C
                dve.wait_ge(m_done, b + 1)
                nc.vector.tensor_tensor(BD[lo:hi, q, lo:hi], m_ps[lo:hi, lo:hi], ident[lo:hi, lo:hi],
                                        ALU.add).then_inc(bd_ready, 1)

            def dve_step(b, q, half, prev=True, pprev=True, last=False):
                row_max(b, 1)
                if pprev:
                    keep_m(b - 2, q, half)
                split_lo(b, 0)
                if not last:
                    row_max(b + 1, 0)
                split_lo(b, 1)
                if prev:
                    divide_r(b - 1)

            row_max(0, 0)
            dve_step(0, 0, 0, prev=False, pprev=False)
            dve_step(1, 0, 1, pprev=False)
            with dve.Fori(1, PAIRS - 1) as j:
                dve_step(j * 2, j - 1, 0)
                dve_step(j * 2 + 1, j - 1, 1)
            dve_step(LAST - 1, PAIRS - 2, 0)
            dve_step(LAST, PAIRS - 2, 1, last=True)
            keep_m(LAST - 1, PAIRS - 1, 0)
            divide_r(LAST)
            keep_m(LAST, PAIRS - 1, 1)

            with dve.Fori(0, PAIRS // 2) as i:
                for s in two:
                    dve.wait_ge(f_done[s], i + 1)
                    nc.vector.tensor_scalar(X[:, i * 2 + s, :], f_ps[s], vec[:, BO_:BO_ + 1], None,
                                            ALU.add).then_inc(x1_ready[s], 1)
                for s in two:
                    dve.wait_ge(y_ready[s], i + 1)
                    for h in two:
                        nc.vector.bn_stats(ST[:, bass.ds(i * 2 + s, 1), h, :].rearrange("p q e -> p (q e)"),
                                           Y[:, i * 2 + s, h * BANK:(h + 1) * BANK]).then_inc(st_ready[s], 1)

            for s in two:
                dve.wait_ge(st_ready[s], PAIRS)
            nc.vector.bn_aggr(MV[:], ST[:].rearrange("p q h e -> p (q h e)")).then_inc(mv_ready, 1)
            dve.wait_ge(fold_done, 1)
            nc.vector.tensor_copy(FS[:], ps[:, 0, 0:3]).then_inc(bn_step, 1)
            dve.wait_ge(bn_step, 1)
            nc.vector.scalar_tensor_tensor(tiny[:, 0:1], FS[:, 2:3], FS[:, 2:3], FS[:, 1:2], op0=ALU.mult,
                                           op1=ALU.add).then_inc(bn_step, 1)
            dve.wait_ge(bn_act, 2)
            nc.vector.tensor_tensor(tiny[:, 3:4], tiny[:, 2:3], vec[:, GA_:GA_ + 1], ALU.mult).then_inc(bn_step, 1)
            dve.wait_ge(bn_step, 3)
            nc.vector.tensor_tensor(tiny[:, 4:5], FS[:, 0:1], tiny[:, 3:4], ALU.mult).then_inc(bn_step, 1)
            dve.wait_ge(bn_step, 4)
            nc.vector.tensor_tensor(tiny[:, 5:6], vec[:, BE_:BE_ + 1], tiny[:, 4:5], ALU.subtract
                                    ).then_inc(affine_ready, 1)
            with dve.Fori(0, PAIRS // 2) as i:
                for s in two:
                    dve.wait_ge(t4_ready[s], i + 1)
                    nc.vector.tensor_tensor(XN[:, i * 2 + s, :], T4[:, s, :], X[:, i * 2 + s, :],
                                            ALU.add).then_inc(o_ready[s], 1)

        @block.tensor
        def _(pe):
            pe.wait_ge(ident_ready, 1)
            pe.wait_ge(wk_loaded, 32)
            for t in range(NT):
                last = nc.tensor.transpose(ps[:, 6, t * P:(t + 1) * P], wk_in[:, t].rearrange("p d i -> p (d i)"),
                                           ident[:])
            last.then_inc(wkt_done, 1)
            pe.wait_ge(w_loaded, 96)
            for t in range(NT):
                last = nc.tensor.transpose(ps[:, 7, t * C:(t + 1) * C], wo_in[:, t * P:(t + 1) * P], ident[0:C, 0:C])
            last.then_inc(wot_done, 1)
            pe.wait_ge(wsign_ready, 2)
            pe.wait_ge(dve_const, 2)
            pe.wait_ge(wkl_ready, 1)
            for k in range(TAPS):
                last = nc.tensor.transpose(xt_ps[0][:, k * C:(k + 1) * C],
                                           wc_sign[:, k].rearrange("o d i -> o (d i)"), ident_bf[0:C, 0:C])
            last.then_inc(ct_done, 1)
            pe.wait_ge(heads_ready, NT * HPT)
            for t in range(NT):
                last = nc.tensor.matmul(ps[:, 7, t * HPT * C:(t + 1) * HPT * C],
                                        wv_in[:, t].rearrange("p d i -> p (d i)"),
                                        wo_heads[:, t].rearrange("p h c -> p (h c)"), start=True, stop=True)
            last.then_inc(u_done, 1)

            pe.wait_ge(mats_ready, 4)
            with pe.Fori(0, PAIRS // 2) as i:
                for s in two:
                    pe.wait_ge(x_loaded[s], (i + 1) * 16)
                    pe.wait_ge(xc_ready[s], i)
                    for h in two:
                        last = nc.tensor.matmul(pc[s][:, h * BANK:(h + 1) * BANK], center_mat[:],
                                                X[:, i * 2 + s, h * BANK:(h + 1) * BANK], start=True, stop=True)
                    last.then_inc(centered[s], 1)
                for s in two:
                    pe.wait_ge(sq_ready[s], i + 1)
                    pe.wait_ge(lnv_ready[1 - s], i + s)
                    for h in two:
                        last = nc.tensor.matmul(pv[:, h * BANK:(h + 1) * BANK], mean_mat[:],
                                                sq[:, s, h * BANK:(h + 1) * BANK], start=True, stop=True)
                    last.then_inc(var_ready[s], 1)
                if True:
                    pe.wait_ge(wct_ready, 2)
                    pe.wait_ge(u_ready, 1)
                for s in two:
                    pe.wait_ge(hi_ready[s], i + 1)
                    pe.wait_ge(lo_ready[s], i + 1)
                    pe.wait_ge(xth_ready[1 - s], i + s)
                    pe.wait_ge(xtl_ready[1 - s], i + s)
                    for part, src in enumerate((x_hi, x_lo)):
                        for k in range(CH):
                            last = nc.tensor.transpose(xt_ps[part][:, k * P:(k + 1) * P],
                                                       src[:, s, k * P:(k + 1) * P], ident_bf[:])
                    last.then_inc(xt_done[s], 1)

            def keys(b, t):
                pe.wait_ge(exp_ready[t], b)
                for w, first in ((wk_hi, True), (wk_lo, False)):
                    for h in two:
                        last = nc.tensor.matmul(k_ps[t][:, h * BANK:(h + 1) * BANK], w[:, t, :],
                                                S[:, bass.ds(b, 1), h * BANK:(h + 1) * BANK]
                                                .rearrange("p b n -> p (b n)"), start=first, stop=not first)
                last.then_inc(k_ready[t], 1)

            def transpose_e(b, t):
                pe.wait_ge(exp_ready[t], b + 1)
                for h in two:
                    pe.wait_ge(etl_ready[h], b * 2 + t)
                    for k in range(CPB):
                        last = nc.tensor.transpose(t_ps[h][:, k * P:(k + 1) * P],
                                                   E[:, t, (h * CPB + k) * P:(h * CPB + k + 1) * P], ident[:])
                    last.then_inc(et_done[h], 1)

            def context(b, t):
                if t == 0:
                    pe.wait_ge(pt_ready, b)
                for h in two:
                    pe.wait_ge(etl_ready[h], b * 2 + t + 1)
                    for k in range(h * CPB, (h + 1) * CPB):
                        for e in (et_hi, et_lo):
                            last = nc.tensor.matmul(d_ps[:, t * P:(t + 1) * P],
                                                    XT[:, bass.ds(b, 1), k].rearrange("p b d c -> p (b d c)"),
                                                    e[:, t, k * P:(k + 1) * P],
                                                    start=(k == 0 and e is et_hi), stop=(k == CH - 1 and e is et_lo))
                last.then_inc(d_done[t], 1)

            def project(b):
                pe.wait_ge(pt_ready, b + 1)
                pe.wait_ge(bd_ready, b)
                for h in range(HEADS):
                    t, g = h // HPT, h % HPT
                    last = nc.tensor.matmul(r_ps[g * DH:(g + 1) * DH, t * C:(t + 1) * C],
                                            PT[:, t, g * DH:(g + 1) * DH], u_all[:, h, :], start=True, stop=True)
                last.then_inc(r_done, 1)

            def matrix(b):
                pe.wait_ge(r_ready, b * 2 + 2)
                for t in range(NT):
                    last = nc.tensor.matmul(m_ps, wq_in[:, t].rearrange("p d i -> p (d i)"),
                                            R[:, t:t + 1, :].broadcast_to([P, 2, C]), start=(t == 0),
                                            stop=(t == NT - 1))
                last.then_inc(m_done, 1)

            def pe_step(b, prev=True, pprev=True, last=False):
                transpose_e(b, 0)
                if pprev:
                    matrix(b - 2)
                if prev:
                    context(b - 1, 1)
                if not last:
                    keys(b + 1, 0)
                transpose_e(b, 1)
                if prev:
                    project(b - 1)
                context(b, 0)
                if not last:
                    keys(b + 1, 1)

            for s in two:
                pe.wait_ge(stacked[s], 64 * (PAIRS // 2))
                pe.wait_ge(xth_ready[s], PAIRS // 2)
                pe.wait_ge(xtl_ready[s], PAIRS // 2)
            keys(0, 0)
            keys(0, 1)
            pe_step(0, prev=False, pprev=False)
            pe_step(1, pprev=False)
            with pe.Fori(2, LAST) as b:
                pe_step(b)
            pe_step(LAST, last=True)
            matrix(LAST - 1)
            context(LAST, 1)
            project(LAST)
            matrix(LAST)

            with pe.Fori(0, PAIRS // 2) as i:
                for s in two:
                    pe.wait_ge(bds_ready[s], i + 1)
                    pe.wait_ge(x1_ready[s], i)
                    for h in two:
                        last = nc.tensor.matmul(f_ps[s][:, h * BANK:(h + 1) * BANK], bd[:, s, :],
                                                XN[:, i * 2 + s, h * BANK:(h + 1) * BANK], start=True, stop=True)
                    last.then_inc(f_done[s], 1)
                for s in two:
                    pe.wait_ge(sg_ready[s], i + 1)
                    pe.wait_ge(y_ready[s], i)
                    for h in two:
                        for k in range(TAPS):
                            r, c = k // 3, k % 3
                            last = nc.tensor.matmul(c_ps[s][:, h * BANK:(h + 1) * BANK], wc_t[:, k, :],
                                                    SG[:, s, h * ROWS + r:h * ROWS + r + ROWS, c:c + W],
                                                    start=(k == 0), stop=(k == TAPS - 1))
                    last.then_inc(conv_done[s], 1)

            pe.wait_ge(mv_ready, 1)
            nc.tensor.matmul(ps[:, 0, 0:2], fold[:].rearrange("p d c -> p (d c)"), MV[:], start=True, stop=True)
            nc.tensor.matmul(ps[:, 0, 2:3], unfold[:], MV[:, 0:1], start=True, stop=True).then_inc(fold_done, 1)


_INS = ["x", "L0_conv_g", "L0_conv_b", "L0_conv_w_qkv", "L0_conv_w_out", "L0_conv_b_out", "L1_conv_W",
        "L1_conv_gamma", "L1_conv_beta"]


def kernel(**inputs):
    import numpy as _np
    import concourse.bacc as _bacc
    from concourse import mybir as _mybir
    from concourse.bass_utils import run_bass_kernel_spmd as _run

    nc = _bacc.Bacc("TRN2", target_bir_lowering=False, num_devices=1)
    arrays, args = {}, []
    for name in _INS:
        a = _np.ascontiguousarray(inputs[name])
        arrays[f"in_{name}"] = a
        args.append(nc.dram_tensor(f"in_{name}", a.shape, _mybir.dt.from_np(a.dtype), kind="ExternalInput").ap())
    shape = _np.shape(inputs["x"])
    out = nc.dram_tensor("out_0", shape, _mybir.dt.float32, kind="ExternalOutput").ap()
    attention_then_binary_conv(nc, *args, out)
    r = _run(nc, [arrays], core_ids=[0])
    return r.results[0]["out_0"]
```

```python
import concourse.bass as bass
from concourse import mybir
from contextlib import ExitStack


def attention_then_binary_conv(nc, x, ln_g, ln_b, w_qkv, w_out, b_out, conv_w, bn_gamma, bn_beta, out):
    f32, bf16, f16 = mybir.dt.float32, mybir.dt.bfloat16, mybir.dt.float16
    ALU, ACT, AX = mybir.AluOpType, mybir.ActivationFunctionType, mybir.AxisListType

    B, C, H, W = x.shape
    P = 128
    N = H * W
    HID = w_out.shape[1]
    DH = 32
    HEADS = HID // DH
    NT = HID // P
    HPT = P // DH
    PAIRS = B // 2
    BANK = 512
    HALVES = N // BANK
    CH = N // P
    CPB = CH // HALVES
    TAPS = conv_w.shape[2] * conv_w.shape[3]
    ROWS = H // HALVES
    SCALE = float(DH) ** -0.5
    LN_EPS = BN_EPS = 1e-5
    LAST = B - 1

    x_d = x.rearrange("(q b) c h w -> q (b c) (h w)", b=2)
    out_d = out.rearrange("(q b) c h w -> q (b c) (h w)", b=2)
    w_d = w_qkv.rearrange("(k t p) i -> k p t i", k=3, p=P)

    with ExitStack() as ctx:
        def sb(name, shape, dt=f32):
            return ctx.enter_context(nc.sbuf_tensor(name, shape, dt))

        def sem(name):
            return ctx.enter_context(nc.semaphore(name))

        ident = sb("ident", [P, P])
        ident_bf = sb("ident_bf", [P, P], bf16)
        mean_mat = sb("mean_mat", [P, P])
        center_mat = sb("center_mat", [P, P])
        fold = sb("fold", [P, 2, C])
        unfold = sb("unfold", [P, P])
        eps = sb("eps", [P, 1])
        wk_in = sb("wk_in", [P, NT, 2, C])
        wq_in = sb("wq_in", [P, NT, 2, C])
        wv_in = sb("wv_in", [P, NT, 2, C])
        wo_in = sb("wo_in", [C, HID])
        wc_in = sb("wc_in", [C, C * TAPS])
        vec_rows = sb("vec_rows", [5, 2, C])
        vec = sb("vec", [P, 5])
        G_, B_, BO_, GA_, BE_ = range(5)
        wk_hi = sb("wk_hi", [P, NT, P], bf16)
        wk_lo = sb("wk_lo", [P, NT, P], bf16)
        wo_heads = sb("wo_heads", [P, NT, HPT, C])
        u_all = sb("u_all", [P, HEADS, C])
        wc_sign = sb("wc_sign", [C, TAPS, 2, C], bf16)
        wc_t = sb("wc_t", [P, 2, 6, C], bf16)

        X = sb("X", [P, PAIRS, N])
        XN = sb("XN", [P, PAIRS, N])
        xc = sb("xc", [P, 2, N])
        sq = sb("sq", [P, 2, N])
        lnv = sb("lnv", [P, 2, N])
        rstd = sb("rstd", [P, 2, N])
        x_hi = sb("x_hi", [P, 2, N], bf16)
        x_lo = sb("x_lo", [P, 2, N], bf16)
        S = sb("S", [P, B, N], bf16)
        XT = sb("XT", [P, B, CH, 2, C], bf16)
        E = sb("E", [P, NT, N])
        et_hi = sb("et_hi", [P, NT, N], bf16)
        et_lo = sb("et_lo", [P, NT, N], bf16)
        negmax = sb("negmax", [P, NT])
        Z = sb("Z", [P, B, NT])
        rz = sb("rz", [P, NT])
        PT = sb("PT", [P, NT, P])
        R = sb("R", [P, NT, C])
        MM = sb("MM", [P, B, 2, C], bf16)
        SG = sb("SG", [P, B, H + 2, W + 2], bf16)
        Y = sb("Y", [P, PAIRS, N], f16)
        ST = sb("ST", [P, PAIRS, HALVES, 6])
        MV = sb("MV", [P, 2])
        FS = sb("FS", [P, 3])
        tiny = sb("tiny", [P, 6])
        T4 = sb("T4", [P, 4, BANK])

        ps = ctx.enter_context(nc.psum_tensor("ps", [P, 8, BANK], f32))

        def banks(a, n=2):
            return ps[:, a:a + n, :].rearrange("p a n -> p (a n)")

        pc = [banks(0), banks(2)]
        pv = banks(4)
        xt_ps = [ps[:, 6, :].bitcast(bf16), ps[:, 7, :].bitcast(bf16)]
        k_ps = [banks(0), banks(2)]
        t_ps = [ps[:, 4, :], ps[:, 5, :]]
        d_ps = ps[:, 6, 0:NT * P]
        r_ps = ps[:, 7, 0:NT * C]
        m_ps = ps[:, 7, 256:256 + P]
        f_ps = [banks(0), banks(2)]
        c_ps = [banks(4), banks(6)]

        two = range(2)
        x_loaded = [sem(f"x_loaded{s}") for s in two]
        wk_loaded, wo_loaded, wc_loaded = sem("wk_loaded"), sem("wo_loaded"), sem("wc_loaded")
        wv_loaded, wq_loaded = sem("wv_loaded"), sem("wq_loaded")
        vec_loaded, vec_ready = sem("vec_loaded"), sem("vec_ready")
        zeroed, ident_ready, mats_ready = sem("zeroed"), sem("ident_ready"), sem("mats_ready")
        dve_const = sem("dve_const")
        wkt_done, wot_done, ct_done, u_done = sem("wkt_done"), sem("wot_done"), sem("ct_done"), sem("u_done")
        wkh_ready, wkl_ready, heads_ready, u_ready, wct_ready = (
            sem("wkh_ready"), sem("wkl_ready"), sem("heads_ready"), sem("u_ready"), sem("wct_ready"))
        wsign_ready = sem("wsign_ready")
        centered = [sem(f"centered{s}") for s in two]
        xc_ready = [sem(f"xc_ready{s}") for s in two]
        sq_ready = [sem(f"sq_ready{s}") for s in two]
        var_ready = [sem(f"var_ready{s}") for s in two]
        lnv_ready = [sem(f"lnv_ready{s}") for s in two]
        rstd_ready = [sem(f"rstd_ready{s}") for s in two]
        scaled = [sem(f"scaled{s}") for s in two]
        xn_ready = [sem(f"xn_ready{s}") for s in two]
        hi_ready = [sem(f"hi_ready{s}") for s in two]
        lo_ready = [sem(f"lo_ready{s}") for s in two]
        stacked = [sem(f"stacked{s}") for s in two]
        xt_done = [sem(f"xt_done{s}") for s in two]
        xth_ready, xtl_ready = [sem(f"xth_ready{s}") for s in two], [sem(f"xtl_ready{s}") for s in two]
        k_ready = [sem(f"k_ready{t}") for t in two]
        max_ready = [sem(f"max_ready{t}") for t in two]
        exp_ready = [sem(f"exp_ready{t}") for t in two]
        et_done = [sem(f"et_done{h}") for h in two]
        eth_ready = [sem(f"eth_ready{h}") for h in two]
        etl_ready = [sem(f"etl_ready{h}") for h in two]
        d_done = [sem(f"d_done{t}") for t in two]
        pt_ready, r_done, rz_ready, r_ready, m_done, mm_ready = (
            sem("pt_ready"), sem("r_done"), sem("rz_ready"), sem("r_ready"), sem("m_done"), sem("mm_ready"))
        f_done = [sem(f"f_done{s}") for s in two]
        x1_ready = sem("x1_ready")
        sg_ready = sem("sg_ready")
        conv_done = [sem(f"conv_done{s}") for s in two]
        y_ready = sem("y_ready")
        st_ready = sem("st_ready")
        mv_ready, fold_done, bn_step, bn_act, affine_ready = (
            sem("mv_ready"), sem("fold_done"), sem("bn_step"), sem("bn_act"), sem("affine_ready"))
        t4_ready = sem("t4_ready")
        o_ready = sem("o_ready")
        stored = sem("stored")
        sg_zeroed = sem("sg_zeroed")
        shifted = [sem(f"shifted{q}") for q in range(PAIRS)]

        block = ctx.enter_context(nc.Block())

        @block.sync
        def _(sp):
            sp.dma_start(X[:, 0, :], x_d[0]).then_inc(x_loaded[0], 16)
            sp.dma_start(X[:, 1, :], x_d[1]).then_inc(x_loaded[1], 16)
            for s in two:
                sp.wait_ge(x_loaded[s], 16)
                sp.dma_start(X[:, 2 + s, :], x_d[2 + s]).then_inc(x_loaded[s], 16)
            for i in range(PAIRS // 2):
                for s in two:
                    q = i * 2 + s
                    sp.wait_ge(stacked[s], i * 64)
                    sp.wait_ge(hi_ready[s], i + 1)
                    sp.dma_start(S[0:C, q * 2, :], x_hi[0:C, s, :]).then_inc(stacked[s], 16)
                    sp.dma_start(S[C:P, q * 2 + 1, :], x_hi[C:P, s, :]).then_inc(stacked[s], 16)
                    sp.wait_ge(lo_ready[s], i + 1)
                    sp.dma_start(S[C:P, q * 2, :], x_lo[0:C, s, :]).then_inc(stacked[s], 16)
                    sp.dma_start(S[0:C, q * 2 + 1, :], x_lo[C:P, s, :]).then_inc(stacked[s], 16)
            for q in range(PAIRS):
                sp.wait_ge(sg_ready, 2 * q + 2)
                sp.dma_start(SG[C:P, 2 * q, 0:H + 1, :], SG[0:C, 2 * q, 1:H + 2, :]).then_inc(shifted[q], 16)
                sp.dma_start(SG[0:C, 2 * q + 1, 0:H + 1, :], SG[C:P, 2 * q + 1, 1:H + 2, :]).then_inc(shifted[q], 16)
            for n in range(PAIRS * HALVES):
                q, h = n // HALVES, n % HALVES
                sp.wait_ge(o_ready, n + 1)
                sp.dma_start(out_d[q, :, h * BANK:(h + 1) * BANK], XN[:, q, h * BANK:(h + 1) * BANK]
                             ).then_inc(stored, 16)
            sp.wait_ge(stored, 16 * PAIRS * HALVES)

        @block.gpsimd
        def _(pool):
            nc.gpsimd.memset(ident[:], 0.0).then_inc(zeroed, 1)
            pool.wait_ge(zeroed, 1)
            nc.gpsimd.affine_select(out=ident[:], in_=ident[:], compare_op=ALU.not_equal, fill=1.0, base=0,
                                    pattern=[[-1, P]], channel_multiplier=1).then_inc(ident_ready, 1)
            nc.gpsimd.memset(wc_t[:], 0.0).then_inc(zeroed, 1)
            nc.gpsimd.memset(wo_heads[:], 0.0).then_inc(zeroed, 1)
            nc.gpsimd.memset(SG[:], 0.0).then_inc(sg_zeroed, 1)
            for i in range(PAIRS // 2):
                for s in two:
                    pool.wait_ge(hi_ready[s], i + 1)
                    pool.wait_ge(xt_done[s], i)
                    pool.wait_ge(stacked[s], i * 64)
                    nc.gpsimd.tensor_tensor(x_lo[:, s, :], XN[:, i * 2 + s, :], x_hi[:, s, :],
                                            ALU.subtract).then_inc(lo_ready[s], 1)

        @block.scalar
        def _(act):
            nc.scalar.preload_act_table_set("natural_log_exp_and_others")
            for i, v in enumerate((ln_g.rearrange("a c h w -> a (c h w)"), ln_b.rearrange("a c h w -> a (c h w)"),
                                   b_out.unsqueeze(0), bn_gamma.unsqueeze(0), bn_beta.unsqueeze(0))):
                act.dma_start(vec_rows[i:i + 1], v.unsqueeze(1).broadcast_to([1, 2, C])).then_inc(vec_loaded, 16)
            for d in two:
                act.dma_start(wk_in[:, :, d, :], w_d[1]).then_inc(wk_loaded, 16)
            act.dma_start(wo_in[:], w_out).then_inc(wo_loaded, 16)
            act.dma_start(wc_in[:], conv_w.rearrange("o i h w -> o (i h w)")).then_inc(wc_loaded, 16)
            for d in two:
                act.dma_start(wv_in[:, :, d, :], w_d[2]).then_inc(wv_loaded, 16)
            for d in two:
                act.dma_start(wq_in[:, :, d, :], w_d[0]).then_inc(wq_loaded, 16)
            def keep_centered(q):
                s, i = q % 2, q // 2
                act.wait_ge(centered[s], i + 1)
                act.wait_ge(scaled[s], i)
                nc.scalar.copy(xc[:, s, :], pc[s]).then_inc(xc_ready[s], 1)

            def inverse_std(q):
                s, i = q % 2, q // 2
                act.wait_ge(var_ready[s], i + 1)
                nc.scalar.activation(lnv[:, s, :], pv, ACT.Ln, bias=eps[:, 0:1]).then_inc(lnv_ready[s], 1)
                act.wait_ge(lnv_ready[s], i + 1)
                act.wait_ge(scaled[s], i)
                nc.scalar.activation(rstd[:, s, :], lnv[:, s, :], ACT.Exp, scale=-0.5).then_inc(rstd_ready[s], 1)

            def keep_xt_hi(q):
                act.wait_ge(xt_done[q % 2], q // 2 + 1)
                nc.scalar.copy(XT[:, 2 * q:2 * q + 2, :, 0, :].rearrange("p b k c -> p k b c"),
                               xt_ps[0].rearrange("p (k b c) -> p k b c", k=CH, b=2)).then_inc(xth_ready[q % 2], 1)

            act.wait_ge(dve_const, 1)
            keep_centered(0)
            keep_centered(1)
            act.wait_ge(wkt_done, 1)
            nc.scalar.copy(wk_hi[:].rearrange("p t c -> p (t c)"), ps[:, 6, 0:NT * P]).then_inc(wkh_ready, 1)
            inverse_std(0)
            keep_centered(2)
            act.wait_ge(wc_loaded, 16)
            for d in two:
                nc.scalar.activation(wc_sign[:, :, d, :].rearrange("o t i -> o i t"),
                                     wc_in[:].rearrange("o (i t) -> o i t", t=TAPS), ACT.Sign).then_inc(wsign_ready, 1)
            inverse_std(1)
            keep_xt_hi(0)
            keep_centered(3)
            inverse_std(2)
            keep_xt_hi(1)
            inverse_std(3)
            keep_xt_hi(2)

            def exp(b, t):
                act.wait_ge(max_ready[t], b + 1)
                if not isinstance(b, int) or b:
                    act.wait_ge(et_done[1], b * 2 + t - 1)
                nc.scalar.activation(E[:, t, :], k_ps[t], ACT.Exp, bias=negmax[:, t:t + 1],
                                     accum_out=Z[:, bass.ds(b, 1), t]).then_inc(exp_ready[t], 1)

            def split_hi(b, t):
                for h in two:
                    act.wait_ge(et_done[h], b * 2 + t + 1)
                    act.wait_ge(d_done[t], b)
                    nc.scalar.copy(et_hi[:, t, h * BANK:(h + 1) * BANK], t_ps[h]).then_inc(eth_ready[h], 1)

            def keep_pt(b):
                act.wait_ge(d_done[1], b + 1)
                act.wait_ge(r_done, b)
                nc.scalar.copy(PT[:].rearrange("p t c -> p (t c)"), d_ps).then_inc(pt_ready, 1)

            def act_step(b, first=False, last=False):
                split_hi(b, 0)
                exp(b, 1)
                if not first:
                    keep_pt(b - 1)
                split_hi(b, 1)
                if not last:
                    exp(b + 1, 0)

            exp(0, 0)
            keep_xt_hi(3)
            act_step(0, first=True)
            act_step(1)
            with act.Fori(2, LAST) as b:
                act_step(b)
            act_step(LAST, last=True)

            def signs(q):
                act.wait_ge(sg_zeroed, 1)
                act.wait_ge(x1_ready, q + 1)
                for d in two:
                    half = slice(d * C, d * C + C)
                    nc.scalar.activation(SG[half, 2 * q + d, 1:H + 1, 1:W + 1],
                                         X[half, q, :].rearrange("p (h w) -> p h w", h=H),
                                         ACT.Sign).then_inc(sg_ready, 1)

            def keep_y(q):
                act.wait_ge(conv_done[q % 2], q // 2 + 1)
                nc.scalar.copy(Y[:, q, :], c_ps[q % 2]).then_inc(y_ready, 1)

            keep_pt(LAST)
            signs(0)
            signs(1)
            signs(2)
            keep_y(0)
            signs(3)
            keep_y(1)
            keep_y(2)
            keep_y(3)

            act.wait_ge(bn_step, 2)
            nc.scalar.activation(tiny[:, 1:2], tiny[:, 0:1], ACT.Ln, bias=eps[:, 0:1]).then_inc(bn_act, 1)
            act.wait_ge(bn_act, 1)
            nc.scalar.activation(tiny[:, 2:3], tiny[:, 1:2], ACT.Exp, scale=-0.5).then_inc(bn_act, 1)
            act.wait_ge(affine_ready, 1)
            for n in range(PAIRS * HALVES):
                q, h = n // HALVES, n % HALVES
                if n >= 4:
                    act.wait_ge(o_ready, n - 3)
                nc.scalar.activation(T4[:, n % 4, :], Y[:, q, h * BANK:(h + 1) * BANK], ACT.Identity,
                                     bias=tiny[:, 5:6], scale=tiny[:, 3:4]).then_inc(t4_ready, 1)

        @block.vector
        def _(dve):
            nc.vector.memset(mean_mat[:], 0.0).then_inc(mats_ready, 1)
            nc.vector.memset(eps[:], LN_EPS).then_inc(dve_const, 1)
            dve.wait_ge(mats_ready, 1)
            for d in two:
                nc.vector.memset(mean_mat[d * C:d * C + C, d * C:d * C + C], 1.0 / C).then_inc(mats_ready, 1)
            dve.wait_ge(ident_ready, 1)
            dve.wait_ge(mats_ready, 3)
            nc.vector.tensor_tensor(center_mat[:], ident[:], mean_mat[:], ALU.subtract).then_inc(mats_ready, 1)
            nc.vector.tensor_copy(ident_bf[:], ident[:]).then_inc(dve_const, 1)
            nc.vector.tensor_tensor(unfold[:, 0:C], ident[:, 0:C], ident[:, C:P], ALU.add).then_inc(dve_const, 1)
            dve.wait_ge(dve_const, 3)
            for d in two:
                nc.vector.tensor_scalar(fold[:, d, :], unfold[:, 0:C], 0.5, None, ALU.mult).then_inc(dve_const, 1)
            dve.wait_ge(dve_const, 5)
            nc.vector.tensor_tensor(unfold[:], ident[:], fold[:].rearrange("p d c -> p (d c)"),
                                    ALU.subtract).then_inc(dve_const, 1)
            def square(q):
                s, i = q % 2, q // 2
                dve.wait_ge(xc_ready[s], i + 1)
                dve.wait_ge(var_ready[s], i)
                nc.vector.tensor_tensor(sq[:, s, :], xc[:, s, :], xc[:, s, :], ALU.mult).then_inc(sq_ready[s], 1)

            def normalise(q):
                s, i = q % 2, q // 2
                dve.wait_ge(rstd_ready[s], i + 1)
                nc.vector.scalar_tensor_tensor(XN[:, q, :], xc[:, s, :], vec[:, G_:G_ + 1], rstd[:, s, :],
                                               op0=ALU.mult, op1=ALU.mult).then_inc(scaled[s], 1)
                dve.wait_ge(scaled[s], i + 1)
                nc.vector.tensor_scalar(XN[:, q, :], XN[:, q, :], vec[:, B_:B_ + 1], None,
                                        ALU.add).then_inc(xn_ready[s], 1)
                dve.wait_ge(xn_ready[s], i + 1)
                dve.wait_ge(xt_done[s], i)
                dve.wait_ge(stacked[s], i * 64)
                dve.wait_ge(lo_ready[s], i)
                nc.vector.tensor_copy(x_hi[:, s, :], XN[:, q, :]).then_inc(hi_ready[s], 1)

            def keep_xt_lo(q):
                dve.wait_ge(xt_done[q % 2], q // 2 + 1)
                nc.vector.tensor_copy(XT[:, 2 * q:2 * q + 2, :, 1, :].rearrange("p b k c -> p k b c"),
                                      xt_ps[1].rearrange("p (k b c) -> p k b c", k=CH, b=2)
                                      ).then_inc(xtl_ready[q % 2], 1)

            square(0)
            square(1)
            dve.wait_ge(wkh_ready, 1)
            nc.vector.tensor_copy(vec[:], ps[:, 6, NT * P:NT * P + 5]).then_inc(vec_ready, 1)
            nc.vector.tensor_tensor(wk_lo[:].rearrange("p t c -> p (t c)"), ps[:, 6, 0:NT * P],
                                    wk_hi[:].rearrange("p t c -> p (t c)"), ALU.subtract).then_inc(wkl_ready, 1)
            dve.wait_ge(wot_done, 1)
            dve.wait_ge(zeroed, 3)
            for t in range(NT):
                for h in range(HPT):
                    nc.vector.tensor_copy(wo_heads[h * DH:(h + 1) * DH, t, h, :],
                                          ps[h * DH:(h + 1) * DH, 7, t * C:(t + 1) * C]).then_inc(heads_ready, 1)
            dve.wait_ge(vec_ready, 1)
            normalise(0)
            square(2)
            dve.wait_ge(u_done, 1)
            nc.vector.tensor_copy(u_all[:].rearrange("p h c -> p (h c)"), ps[:, 7, :]).then_inc(u_ready, 1)
            dve.wait_ge(ct_done, 1)
            taps = xt_ps[0][:, 0:TAPS * C].rearrange("p (r k c) -> p r k c", r=3, c=C)
            for d in two:
                own, ahead = slice(d * C, d * C + C), slice(C - d * C, P - d * C)
                nc.vector.tensor_copy(wc_t[own, d, 0:3, :], taps[own, 0]).then_inc(wct_ready, 1)
                nc.vector.tensor_copy(wc_t[ahead, d, 0:3, :], taps[ahead, 1]).then_inc(wct_ready, 1)
                nc.vector.tensor_copy(wc_t[ahead, d, 3:6, :], taps[ahead, 2]).then_inc(wct_ready, 1)
            normalise(1)
            keep_xt_lo(0)
            square(3)
            normalise(2)
            keep_xt_lo(1)
            normalise(3)
            keep_xt_lo(2)

            def row_max(b, t):
                dve.wait_ge(k_ready[t], b + 1)
                nc.vector.tensor_reduce(negmax[:, t:t + 1], k_ps[t], AX.X, ALU.max, negate=True
                                        ).then_inc(max_ready[t], 1)

            def split_lo(b, t):
                for h in two:
                    dve.wait_ge(eth_ready[h], b * 2 + t + 1)
                    dve.wait_ge(d_done[t], b)
                    nc.vector.tensor_tensor(et_lo[:, t, h * BANK:(h + 1) * BANK], t_ps[h],
                                            et_hi[:, t, h * BANK:(h + 1) * BANK], ALU.subtract
                                            ).then_inc(etl_ready[h], 1)

            def divide_r(b):
                dve.wait_ge(exp_ready[1], b + 1)
                dve.wait_ge(exp_ready[0], b + 1)
                nc.vector.reciprocal(rz[:], Z[:, bass.ds(b, 1), :].rearrange("p b t -> p (b t)")).then_inc(rz_ready, 1)
                dve.wait_ge(rz_ready, b + 1)
                dve.wait_ge(r_done, b + 1)
                dve.wait_ge(m_done, b)
                for t in range(NT):
                    nc.vector.tensor_scalar(R[:, t, :], r_ps[:, t * C:(t + 1) * C], rz[:, t:t + 1], SCALE,
                                            ALU.mult, ALU.mult).then_inc(r_ready, 1)

            def split_m(b):
                dve.wait_ge(m_done, b + 1)
                hi, lo = (MM[:, bass.ds(b, 1), e, :].rearrange("p b c -> p (b c)") for e in two)
                nc.vector.tensor_scalar(hi, m_ps[:, 0:C], 1.0, None, ALU.mult).then_inc(mm_ready, 1)
                dve.wait_ge(mm_ready, b * 2 + 1)
                nc.vector.tensor_tensor(lo, m_ps[:, 0:C], hi, ALU.subtract).then_inc(mm_ready, 1)

            def dve_step(b, prev=True, pprev=True, last=False):
                row_max(b, 1)
                if pprev:
                    split_m(b - 2)
                split_lo(b, 0)
                if not last:
                    row_max(b + 1, 0)
                split_lo(b, 1)
                if prev:
                    divide_r(b - 1)

            row_max(0, 0)
            keep_xt_lo(3)
            dve_step(0, prev=False, pprev=False)
            dve_step(1, pprev=False)
            with dve.Fori(2, LAST) as b:
                dve_step(b)
            def add_input(q):
                dve.wait_ge(f_done[q % 2], q // 2 + 1)
                nc.vector.scalar_tensor_tensor(X[:, q, :], f_ps[q % 2], vec[:, BO_:BO_ + 1], XN[:, q, :],
                                               op0=ALU.add, op1=ALU.add).then_inc(x1_ready, 1)

            def statistics(q):
                dve.wait_ge(y_ready, q + 1)
                for h in range(HALVES):
                    nc.vector.bn_stats(ST[:, q, h, :], Y[:, q, h * BANK:(h + 1) * BANK]).then_inc(st_ready, 1)

            dve_step(LAST, last=True)
            add_input(0)
            split_m(LAST - 1)
            add_input(1)
            divide_r(LAST)
            add_input(2)
            split_m(LAST)
            add_input(3)
            for q in range(PAIRS):
                statistics(q)

            dve.wait_ge(st_ready, PAIRS * HALVES)
            nc.vector.bn_aggr(MV[:], ST[:].rearrange("p q h e -> p (q h e)")).then_inc(mv_ready, 1)
            dve.wait_ge(fold_done, 1)
            nc.vector.tensor_copy(FS[:], ps[:, 0, 0:3]).then_inc(bn_step, 1)
            dve.wait_ge(bn_step, 1)
            nc.vector.scalar_tensor_tensor(tiny[:, 0:1], FS[:, 2:3], FS[:, 2:3], FS[:, 1:2], op0=ALU.mult,
                                           op1=ALU.add).then_inc(bn_step, 1)
            dve.wait_ge(bn_act, 2)
            nc.vector.tensor_tensor(tiny[:, 3:4], tiny[:, 2:3], vec[:, GA_:GA_ + 1], ALU.mult).then_inc(bn_step, 1)
            dve.wait_ge(bn_step, 3)
            nc.vector.tensor_tensor(tiny[:, 4:5], FS[:, 0:1], tiny[:, 3:4], ALU.mult).then_inc(bn_step, 1)
            dve.wait_ge(bn_step, 4)
            nc.vector.tensor_tensor(tiny[:, 5:6], vec[:, BE_:BE_ + 1], tiny[:, 4:5], ALU.subtract
                                    ).then_inc(affine_ready, 1)
            for n in range(PAIRS * HALVES):
                q, h = n // HALVES, n % HALVES
                part = slice(h * BANK, (h + 1) * BANK)
                dve.wait_ge(t4_ready, n + 1)
                nc.vector.tensor_tensor(XN[:, q, part], T4[:, n % 4, :], X[:, q, part], ALU.add).then_inc(o_ready, 1)

        @block.tensor
        def _(pe):
            pe.wait_ge(mats_ready, 4)
            def center(q):
                s, i = q % 2, q // 2
                pe.wait_ge(x_loaded[s], (i + 1) * 16)
                pe.wait_ge(xc_ready[s], i)
                for h in range(HALVES):
                    last = nc.tensor.matmul(pc[s][:, h * BANK:(h + 1) * BANK], center_mat[:],
                                            X[:, q, h * BANK:(h + 1) * BANK], start=True, stop=True)
                last.then_inc(centered[s], 1)

            def variance(q):
                s, i = q % 2, q // 2
                pe.wait_ge(sq_ready[s], i + 1)
                if q:
                    pe.wait_ge(lnv_ready[1 - s], (q - 1) // 2 + 1)
                for h in range(HALVES):
                    last = nc.tensor.matmul(pv[:, h * BANK:(h + 1) * BANK], mean_mat[:],
                                            sq[:, s, h * BANK:(h + 1) * BANK], start=True, stop=True)
                last.then_inc(var_ready[s], 1)

            def transpose_x(q):
                s, i = q % 2, q // 2
                pe.wait_ge(hi_ready[s], i + 1)
                pe.wait_ge(lo_ready[s], i + 1)
                if q:
                    pe.wait_ge(xth_ready[1 - s], (q - 1) // 2 + 1)
                    pe.wait_ge(xtl_ready[1 - s], (q - 1) // 2 + 1)
                for part, src in enumerate((x_hi, x_lo)):
                    for k in range(CH):
                        last = nc.tensor.transpose(xt_ps[part][:, k * P:(k + 1) * P],
                                                   src[:, s, k * P:(k + 1) * P], ident_bf[:])
                last.then_inc(xt_done[s], 1)

            center(0)
            center(1)
            pe.wait_ge(vec_loaded, 80)
            nc.tensor.transpose(ps[:, 6, NT * P:NT * P + 5], vec_rows[:].rearrange("v d c -> v (d c)"),
                                ident[0:5, 0:5])
            pe.wait_ge(wk_loaded, 32)
            for t in range(NT):
                last = nc.tensor.transpose(ps[:, 6, t * P:(t + 1) * P], wk_in[:, t].rearrange("p d i -> p (d i)"),
                                           ident[:])
            last.then_inc(wkt_done, 1)
            pe.wait_ge(wo_loaded, 16)
            for t in range(NT):
                last = nc.tensor.transpose(ps[:, 7, t * C:(t + 1) * C], wo_in[:, t * P:(t + 1) * P], ident[0:C, 0:C])
            last.then_inc(wot_done, 1)
            variance(0)
            center(2)
            pe.wait_ge(wv_loaded, 32)
            pe.wait_ge(heads_ready, NT * HPT)
            for t in range(NT):
                last = nc.tensor.matmul(ps[:, 7, t * HPT * C:(t + 1) * HPT * C],
                                        wv_in[:, t].rearrange("p d i -> p (d i)"),
                                        wo_heads[:, t].rearrange("p h c -> p (h c)"), start=True, stop=True)
            last.then_inc(u_done, 1)
            pe.wait_ge(wsign_ready, 2)
            pe.wait_ge(dve_const, 2)
            pe.wait_ge(wkl_ready, 1)
            for k in range(TAPS):
                last = nc.tensor.transpose(xt_ps[0][:, k * C:(k + 1) * C],
                                           wc_sign[:, k].rearrange("o d i -> o (d i)"), ident_bf[0:C, 0:C])
            last.then_inc(ct_done, 1)
            variance(1)
            pe.wait_ge(wct_ready, 6)
            pe.wait_ge(u_ready, 1)
            transpose_x(0)
            center(3)
            variance(2)
            transpose_x(1)
            variance(3)
            transpose_x(2)

            def keys(b, t):
                pe.wait_ge(exp_ready[t], b)
                for w, first in ((wk_hi, True), (wk_lo, False)):
                    for h in two:
                        last = nc.tensor.matmul(k_ps[t][:, h * BANK:(h + 1) * BANK], w[:, t, :],
                                                S[:, bass.ds(b, 1), h * BANK:(h + 1) * BANK]
                                                .rearrange("p b n -> p (b n)"), start=first, stop=not first)
                last.then_inc(k_ready[t], 1)

            def transpose_e(b, t):
                pe.wait_ge(exp_ready[t], b + 1)
                for h in two:
                    pe.wait_ge(etl_ready[h], b * 2 + t)
                    for k in range(CPB):
                        last = nc.tensor.transpose(t_ps[h][:, k * P:(k + 1) * P],
                                                   E[:, t, (h * CPB + k) * P:(h * CPB + k + 1) * P], ident[:])
                    last.then_inc(et_done[h], 1)

            def context(b, t):
                if t == 0:
                    pe.wait_ge(pt_ready, b)
                for h in two:
                    pe.wait_ge(etl_ready[h], b * 2 + t + 1)
                    for k in range(h * CPB, (h + 1) * CPB):
                        for e in (et_hi, et_lo):
                            last = nc.tensor.matmul(d_ps[:, t * P:(t + 1) * P],
                                                    XT[:, bass.ds(b, 1), k].rearrange("p b d c -> p (b d c)"),
                                                    e[:, t, k * P:(k + 1) * P],
                                                    start=(k == 0 and e is et_hi), stop=(k == CH - 1 and e is et_lo))
                last.then_inc(d_done[t], 1)

            def project(b):
                pe.wait_ge(pt_ready, b + 1)
                pe.wait_ge(mm_ready, b * 2)
                for h in range(HEADS):
                    t, g = h // HPT, h % HPT
                    last = nc.tensor.matmul(r_ps[g * DH:(g + 1) * DH, t * C:(t + 1) * C],
                                            PT[:, t, g * DH:(g + 1) * DH], u_all[:, h, :], start=True, stop=True)
                last.then_inc(r_done, 1)

            def matrix(b):
                pe.wait_ge(r_ready, b * 2 + 2)
                for t in range(NT):
                    last = nc.tensor.matmul(m_ps, wq_in[:, t].rearrange("p d i -> p (d i)"),
                                            R[:, t:t + 1, :].broadcast_to([P, 2, C]), start=(t == 0),
                                            stop=(t == NT - 1))
                last.then_inc(m_done, 1)

            def pe_step(b, prev=True, pprev=True, last=False):
                transpose_e(b, 0)
                if pprev:
                    matrix(b - 2)
                if prev:
                    context(b - 1, 1)
                if not last:
                    keys(b + 1, 0)
                transpose_e(b, 1)
                if prev:
                    project(b - 1)
                context(b, 0)
                if not last:
                    keys(b + 1, 1)

            pe.wait_ge(wkl_ready, 1)
            pe.wait_ge(stacked[0], 64)
            pe.wait_ge(xc_ready[0], 2)
            keys(0, 0)
            pe.wait_ge(xc_ready[1], 2)
            keys(0, 1)
            transpose_x(3)
            pe.wait_ge(wq_loaded, 32)
            for s in two:
                pe.wait_ge(lnv_ready[s], 2)
                pe.wait_ge(xth_ready[s], 2)
                pe.wait_ge(xtl_ready[s], 2)
            pe_step(0, prev=False, pprev=False)
            for s in two:
                pe.wait_ge(stacked[s], 128)
            pe_step(1, pprev=False)
            with pe.Fori(2, LAST) as b:
                pe_step(b)
            def apply_matrix(q):
                pe.wait_ge(mm_ready, 4 * q + 4)
                pe.wait_ge(x1_ready, max(q - 1, 0))
                for h in range(HALVES):
                    for e in two:
                        for d in two:
                            last = nc.tensor.matmul(f_ps[q % 2][d * C:d * C + C, h * BANK:(h + 1) * BANK],
                                                    MM[:, 2 * q + d, e, :],
                                                    S[:, 2 * q + d, h * BANK:(h + 1) * BANK],
                                                    start=(e == 0), stop=(e == 1))
                last.then_inc(f_done[q % 2], 1)

            def convolve(q):
                pe.wait_ge(shifted[q], 32)
                pe.wait_ge(sg_ready, 2 * q + 2)
                pe.wait_ge(y_ready, max(q - 1, 0))
                for h in range(HALVES):
                    for k in range(6):
                        r, c = h * ROWS + k // 3, k % 3
                        for d in two:
                            last = nc.tensor.matmul(c_ps[q % 2][d * C:d * C + C, h * BANK:(h + 1) * BANK],
                                                    wc_t[:, d, k, :], SG[:, 2 * q + d, r:r + ROWS, c:c + W],
                                                    start=(k == 0), stop=(k == 5))
                last.then_inc(conv_done[q % 2], 1)

            pe_step(LAST, last=True)
            pe.wait_ge(exp_ready[0], B)
            apply_matrix(0)
            context(LAST, 1)
            matrix(LAST - 1)
            pe.wait_ge(exp_ready[1], B)
            apply_matrix(1)
            project(LAST)
            apply_matrix(2)
            for h in two:
                pe.wait_ge(etl_ready[h], B * NT)
            convolve(0)
            matrix(LAST)
            apply_matrix(3)
            pe.wait_ge(pt_ready, B)
            pe.wait_ge(mm_ready, 2 * B)
            convolve(1)
            convolve(2)
            convolve(3)

            pe.wait_ge(mv_ready, 1)
            nc.tensor.matmul(ps[:, 0, 0:2], fold[:].rearrange("p d c -> p (d c)"), MV[:], start=True, stop=True)
            nc.tensor.matmul(ps[:, 0, 2:3], unfold[:], MV[:, 0:1], start=True, stop=True).then_inc(fold_done, 1)


_INS = ["x", "L0_conv_g", "L0_conv_b", "L0_conv_w_qkv", "L0_conv_w_out", "L0_conv_b_out", "L1_conv_W",
        "L1_conv_gamma", "L1_conv_beta"]


def kernel(**inputs):
    import numpy as _np
    import concourse.bacc as _bacc
    from concourse import mybir as _mybir
    from concourse.bass_utils import run_bass_kernel_spmd as _run

    nc = _bacc.Bacc("TRN2", target_bir_lowering=False, num_devices=1)
    arrays, args = {}, []
    for name in _INS:
        a = _np.ascontiguousarray(inputs[name])
        arrays[f"in_{name}"] = a
        args.append(nc.dram_tensor(f"in_{name}", a.shape, _mybir.dt.from_np(a.dtype), kind="ExternalInput").ap())
    shape = _np.shape(inputs["x"])
    out = nc.dram_tensor("out_0", shape, _mybir.dt.float32, kind="ExternalOutput").ap()
    attention_then_binary_conv(nc, *args, out)
    r = _run(nc, [arrays], core_ids=[0])
    return r.results[0]["out_0"]
```

```python
import concourse.bass as bass
from concourse import mybir
from contextlib import ExitStack


def attention_then_binary_conv(nc, x, ln_g, ln_b, w_qkv, w_out, b_out, conv_w, bn_gamma, bn_beta, out):
    f32, bf16, f16 = mybir.dt.float32, mybir.dt.bfloat16, mybir.dt.float16
    ALU, ACT, AX = mybir.AluOpType, mybir.ActivationFunctionType, mybir.AxisListType

    B, C, H, W = x.shape
    P = 128
    N = H * W
    HID = w_out.shape[1]
    DH = 32
    HEADS = HID // DH
    NT = HID // P
    HPT = P // DH
    PAIRS = B // 2
    BANK = 512
    HALVES = N // BANK
    UNITS = PAIRS * HALVES
    CH = N // P
    CPB = CH // HALVES
    TAPS = conv_w.shape[2] * conv_w.shape[3]
    ROWS = H // HALVES
    SCALE = float(DH) ** -0.5
    LN_EPS = BN_EPS = 1e-5
    LAST = B - 1
    OUT_PARTS = [(n // HALVES, slice(n % HALVES * BANK, (n % HALVES + 1) * BANK)) for n in range(PAIRS * HALVES)]
    POOL_PARTS = (3, 6)
    XT_BY_DVE = (1, 3)
    WARM = 7

    x_d = x.rearrange("(q b) c h w -> q (b c) (h w)", b=2)
    out_d = out.rearrange("(q b) c h w -> q (b c) (h w)", b=2)
    w_d = w_qkv.rearrange("(k t p) i -> k p t i", k=3, p=P)

    with ExitStack() as ctx:
        def sb(name, shape, dt=f32):
            return ctx.enter_context(nc.sbuf_tensor(name, shape, dt))

        def sem(name):
            return ctx.enter_context(nc.semaphore(name))

        ident = sb("ident", [P, P])
        ident_bf = sb("ident_bf", [P, P], bf16)
        mean_mat = sb("mean_mat", [P, P])
        center_mat = sb("center_mat", [P, P])
        fold = sb("fold", [P, 2, C])
        fold_neg = sb("fold_neg", [P, 2, C])
        unfold = sb("unfold", [P, P])
        eps = sb("eps", [P, 1])
        wk_in = sb("wk_in", [P, NT, 2, C])
        wq_in = sb("wq_in", [P, NT, 2, C])
        wv_in = sb("wv_in", [P, NT, 2, C])
        wo_in = sb("wo_in", [C, HID])
        wc_in = sb("wc_in", [C, C * TAPS])
        vec_rows = sb("vec_rows", [5, 2, C])
        vec = sb("vec", [P, 6])
        G_, B_, BO_, GA_, BE_, BS_ = range(6)
        wk_hi = sb("wk_hi", [P, NT, P], bf16)
        wk_lo = sb("wk_lo", [P, NT, P], bf16)
        wo_heads = sb("wo_heads", [P, NT, HPT, C])
        u_all = sb("u_all", [P, HEADS, C])
        wc_above = sb("wc_above", [C, C * TAPS])
        wc_below = sb("wc_below", [C, C * TAPS])
        wc_sign = sb("wc_sign", [C, TAPS, 2, C], bf16)
        wc_flat = sb("wc_flat", [P, TAPS, C], bf16)
        wc_t = sb("wc_t", [P, 2, 6, C], bf16)

        X = sb("X", [P, PAIRS, N])
        XN = sb("XN", [P, PAIRS, N])
        sq = sb("sq", [P, 2, BANK])
        lnv = sb("lnv", [P, 2, BANK])
        rstd = sb("rstd", [P, 2, BANK])
        x_hi = sb("x_hi", [P, 2, N], bf16)
        x_lo = sb("x_lo", [P, 2, N], bf16)
        S = sb("S", [P, B, N], bf16)
        XT = sb("XT", [P, B, CH, 2, C], bf16)
        XT_ring = sb("XT_ring", [P, 2, CH, 2, C], bf16)
        E = sb("E", [P, NT, N])
        et_hi = sb("et_hi", [P, NT, N], bf16)
        et_lo = sb("et_lo", [P, NT, N], bf16)
        negmax = sb("negmax", [P, NT])
        Z = sb("Z", [P, B, NT])
        rz = sb("rz", [P, NT])
        PT = sb("PT", [P, NT, P])
        R = sb("R", [P, NT, 2, C])
        MM = sb("MM", [P, B, 2, C], bf16)
        SG = sb("SG", [P, B, H + 2, W + 2], bf16)
        Y = sb("Y", [P, N], f16)
        ST = sb("ST", [P, PAIRS, HALVES, 6])
        MV = sb("MV", [P, 2])
        bn = sb("bn", [P, 5])
        BN_SPREAD, BN_LN, BN_INV, BN_SCALE, BN_SHIFT = (slice(i, i + 1) for i in range(5))

        ps = ctx.enter_context(nc.psum_tensor("ps", [P, 8, BANK], f32))

        def banks(a, n=2):
            return ps[:, a:a + n, :].rearrange("p a n -> p (a n)")

        pc = [ps[:, n, :] for n in range(4)]
        pv = [ps[:, 4, :], ps[:, 5, :]]
        xt_ps = [ps[:, 6, :].bitcast(bf16), ps[:, 7, :].bitcast(bf16)]
        k_ps = [banks(0), banks(2)]
        t_ps = [ps[:, 4, :], ps[:, 5, :]]
        d_ps = ps[:, 6, 0:NT * P]
        r_ps = ps[:, 7, 0:NT * C]
        m_ps = ps[:, 7, BANK // 2:BANK // 2 + P]
        f_ps = [banks(0), banks(2)]
        c_ps = [banks(4), banks(6), banks(0), banks(2)]
        fs_ps = ps[:, 4, 0:3]

        two = range(2)
        x_loaded = [sem(f"x_loaded{n}") for n in range(PAIRS + 1)]
        wk_loaded, wo_loaded, wc_loaded = sem("wk_loaded"), sem("wo_loaded"), sem("wc_loaded")
        wv_loaded, wq_loaded = sem("wv_loaded"), sem("wq_loaded")
        vec_loaded, vec_ready = sem("vec_loaded"), sem("vec_ready")
        ident_zeroed, ident_ready, mats_ready = sem("ident_zeroed"), sem("ident_ready"), sem("mats_ready")
        heads_zeroed, wct_zeroed = sem("heads_zeroed"), sem("wct_zeroed")
        dve_const = sem("dve_const")
        wkt_done, wot_done, ct_done, u_done = sem("wkt_done"), sem("wot_done"), sem("ct_done"), sem("u_done")
        wkh_ready, wkl_ready, heads_ready, u_ready, wct_ready = (
            sem("wkh_ready"), sem("wkl_ready"), sem("heads_ready"), sem("u_ready"), sem("wct_ready"))
        ct_kept = sem("ct_kept")
        wc_compared, wsign_ready = sem("wc_compared"), sem("wsign_ready")
        centered, squared, var_done, lnv_ready, rstd_ready = (
            sem("centered"), sem("squared"), sem("var_done"), sem("lnv_ready"), sem("rstd_ready"))
        scaled, hi_ready, lo_ready, xt_done = sem("scaled"), sem("hi_ready"), sem("lo_ready"), sem("xt_done")
        stacked = [sem(f"stacked{q}") for q in range(PAIRS)]
        xt_kept = [sem(f"xt_kept{s}") for s in two]
        k_ready = [sem(f"k_ready{t}") for t in two]
        max_ready = [sem(f"max_ready{t}") for t in two]
        exp_ready = [sem(f"exp_ready{t}") for t in two]
        et_done = [sem(f"et_done{h}") for h in two]
        eth_ready = [sem(f"eth_ready{h}") for h in two]
        etl_ready = [sem(f"etl_ready{h}") for h in two]
        d_done = [sem(f"d_done{t}") for t in two]
        pt_ready, r_done, rz_ready, r_ready, m_done, mm_ready = (
            sem("pt_ready"), sem("r_done"), sem("rz_ready"), sem("r_ready"), sem("m_done"), sem("mm_ready"))
        f_done = [sem(f"f_done{s}") for s in two]
        x1_ready = sem("x1_ready")
        sg_ready = sem("sg_ready")
        ring_ready = [sem(f"ring_ready{s}") for s in two]
        conv_done = sem("conv_done")
        y_ready = sem("y_ready")
        st_ready = sem("st_ready")
        mv_ready, fold_done, bn_act, scale_ready, affine_ready = (
            sem("mv_ready"), sem("fold_done"), sem("bn_act"), sem("scale_ready"), sem("affine_ready"))
        t_ready = sem("t_ready")
        o_dve, o_pool = sem("o_dve"), sem("o_pool")
        stored = sem("stored")
        sg_zeroed = sem("sg_zeroed")
        shifted = [sem(f"shifted{q}") for q in range(PAIRS)]

        block = ctx.enter_context(nc.Block())

        @block.sync
        def _(sp):
            for h in range(HALVES):
                sp.dma_start(X[:, 0, h * BANK:(h + 1) * BANK], x_d[0, :, h * BANK:(h + 1) * BANK]
                             ).then_inc(x_loaded[h], 16)
            for i, v in enumerate((ln_g.rearrange("a c h w -> a (c h w)"), ln_b.rearrange("a c h w -> a (c h w)"),
                                   b_out.unsqueeze(0), bn_gamma.unsqueeze(0), bn_beta.unsqueeze(0))):
                sp.dma_start(vec_rows[i:i + 1], v.unsqueeze(1).broadcast_to([1, 2, C])).then_inc(vec_loaded, 16)
            for q in range(1, PAIRS):
                if q == 2:
                    sp.wait_ge(centered, 1)
                sp.dma_start(X[:, q, :], x_d[q]).then_inc(x_loaded[q + 1], 16)
            for q in range(PAIRS):
                sp.wait_ge(hi_ready, 2 * q + 2)
                sp.dma_start(S[0:C, q * 2, :], x_hi[0:C, q % 2, :]).then_inc(stacked[q], 16)
                sp.dma_start(S[C:P, q * 2 + 1, :], x_hi[C:P, q % 2, :]).then_inc(stacked[q], 16)
                sp.wait_ge(lo_ready, 2 * q + 2)
                sp.dma_start(S[C:P, q * 2, :], x_lo[0:C, q % 2, :]).then_inc(stacked[q], 16)
                sp.dma_start(S[0:C, q * 2 + 1, :], x_lo[C:P, q % 2, :]).then_inc(stacked[q], 16)
            for b in range(1, LAST - 1):
                for s in two:
                    sp.wait_ge(xt_kept[s], b // 2 + 1)
                if b >= 3:
                    sp.wait_ge(d_done[1], b - 1)
                sp.dma_start(XT_ring[:, b % 2], XT[:, b]).then_inc(ring_ready[b % 2], 16)
            for q in range(PAIRS):
                sp.wait_ge(sg_ready, 2 * q + 1)
                sp.dma_start(SG[C:P, 2 * q, 0:H + 1, :], SG[0:C, 2 * q, 1:H + 2, :]).then_inc(shifted[q], 16)
                sp.wait_ge(sg_ready, 2 * q + 2)
                sp.dma_start(SG[0:C, 2 * q + 1, 0:H + 1, :], SG[C:P, 2 * q + 1, 1:H + 2, :]).then_inc(shifted[q], 16)
            for n, (q, part) in enumerate(OUT_PARTS):
                by_pool = n in POOL_PARTS
                sp.wait_ge(o_pool if by_pool else o_dve, sum((m in POOL_PARTS) == by_pool for m in range(n + 1)))
                sp.dma_start(out_d[q, :, part], XN[:, q, part]).then_inc(stored, 16)
            sp.wait_ge(stored, 16 * len(OUT_PARTS))

        @block.gpsimd
        def _(pool):
            nc.gpsimd.memset(ident[:], 0.0).then_inc(ident_zeroed, 1)
            pool.wait_ge(ident_zeroed, 1)
            nc.gpsimd.affine_select(out=ident[:], in_=ident[:], compare_op=ALU.not_equal, fill=1.0, base=0,
                                    pattern=[[-1, P]], channel_multiplier=1).then_inc(ident_ready, 1)
            for d in two:
                pool.dma_start(wk_in[:, :, d, :], w_d[1]).then_inc(wk_loaded, 16)
            pool.dma_start(wo_in[:], w_out).then_inc(wo_loaded, 16)
            pool.dma_start(wc_in[:], conv_w.rearrange("o i h w -> o (i h w)")).then_inc(wc_loaded, 16)
            for d in two:
                pool.dma_start(wv_in[:, :, d, :], w_d[2]).then_inc(wv_loaded, 16)
            for d in two:
                pool.dma_start(wq_in[:, :, d, :], w_d[0]).then_inc(wq_loaded, 16)
            pool.wait_ge(wc_loaded, 16)
            nc.gpsimd.tensor_scalar(wc_above[:], wc_in[:], 0.0, None, ALU.is_gt).then_inc(wc_compared, 1)
            nc.gpsimd.tensor_scalar(wc_below[:], wc_in[:], 0.0, None, ALU.is_lt).then_inc(wc_compared, 1)
            pool.wait_ge(wc_compared, 2)
            for d in two:
                nc.gpsimd.tensor_tensor(wc_sign[:, :, d, :].rearrange("o t i -> o i t"),
                                        wc_above[:].rearrange("o (i t) -> o i t", t=TAPS),
                                        wc_below[:].rearrange("o (i t) -> o i t", t=TAPS), ALU.subtract
                                        ).then_inc(wsign_ready, 1)
            nc.gpsimd.memset(SG[:, :, 0:H + 2:H + 1, :], 0.0).then_inc(sg_zeroed, 1)
            pool.wait_ge(sg_zeroed, 1)
            nc.gpsimd.memset(SG[:, :, :, 0:W + 2:W + 1], 0.0).then_inc(sg_zeroed, 1)
            pool.wait_ge(ct_kept, 1)
            pool.wait_ge(wct_zeroed, 1)
            pool.wait_ge(sg_zeroed, 2)
            copied = 0
            for d in two:
                own, ahead = slice(d * C, d * C + C), slice(C - d * C, P - d * C)
                for half, place, row in ((own, 0, 0), (ahead, 0, 1), (ahead, 3, 2)):
                    if copied:
                        pool.wait_ge(wct_ready, copied)
                    nc.gpsimd.tensor_copy(wc_t[half, d, place:place + 3, :], wc_flat[half, 3 * row:3 * row + 3]
                                          ).then_inc(wct_ready, 1)
                    copied += 1
            pool.wait_ge(wct_ready, copied)
            for n in POOL_PARTS:
                q, part = OUT_PARTS[n]
                pool.wait_ge(t_ready, n + 1)
                nc.gpsimd.tensor_tensor(XN[:, q, part], XN[:, q, part], X[:, q, part], ALU.add).then_inc(o_pool, 1)

        @block.scalar
        def _(act):
            nc.scalar.preload_act_table_set("natural_log_exp_and_others")
            def square(n):
                act.wait_ge(centered, n + 1)
                if n >= 2:
                    act.wait_ge(var_done, n - 1)
                nc.scalar.activation(sq[:, n % 2, :], pc[n % 4], ACT.Square).then_inc(squared, 1)

            def inverse_std(n):
                act.wait_ge(var_done, n + 1)
                nc.scalar.activation(lnv[:, n % 2, :], pv[n % 2], ACT.Ln, bias=eps[:, 0:1]).then_inc(lnv_ready, 1)
                act.wait_ge(lnv_ready, n + 1)
                if n >= 2:
                    act.wait_ge(scaled, n - 1)
                nc.scalar.activation(rstd[:, n % 2, :], lnv[:, n % 2, :], ACT.Exp, scale=-0.5).then_inc(rstd_ready, 1)

            def keep_xt(n):
                q, h = n // HALVES, n % HALVES
                act.wait_ge(xt_done, n + 1)
                nc.scalar.copy(XT[:, 2 * q:2 * q + 2, h * CPB:(h + 1) * CPB].rearrange("p b k e c -> p (k e) b c"),
                               xt_ps[n % 2].rearrange("p (k b c) -> p k b c", b=2, c=C)).then_inc(xt_kept[n % 2], 1)

            act.wait_ge(dve_const, 1)
            square(0)
            square(1)
            inverse_std(0)
            act.wait_ge(wot_done, 1)
            act.wait_ge(heads_zeroed, 1)
            for g in range(HPT):
                rows = slice(g * DH, (g + 1) * DH)
                nc.scalar.copy(wo_heads[rows, :, g, :], ps[rows, 7, 0:NT * C].rearrange("p (t c) -> p t c", c=C)
                               ).then_inc(heads_ready, 1)
            for n in range(UNITS):
                if n > 0:
                    inverse_std(n)
                if n + 2 < UNITS:
                    square(n + 2)
                if n >= 2 and n - 2 not in XT_BY_DVE and n < UNITS - 1:
                    keep_xt(n - 2)

            def exp(b, t):
                act.wait_ge(max_ready[t], b + 1)
                if not isinstance(b, int) or b:
                    act.wait_ge(et_done[1], b * 2 + t - 1)
                nc.scalar.activation(E[:, t, :], k_ps[t], ACT.Exp, bias=negmax[:, t:t + 1],
                                     accum_out=Z[:, bass.ds(b, 1), t]).then_inc(exp_ready[t], 1)

            def split_hi(b, t):
                for h in two:
                    act.wait_ge(et_done[h], b * 2 + t + 1)
                    act.wait_ge(d_done[t], b)
                    nc.scalar.copy(et_hi[:, t, h * BANK:(h + 1) * BANK], t_ps[h]).then_inc(eth_ready[h], 1)

            def keep_pt(b):
                act.wait_ge(d_done[1], b + 1)
                act.wait_ge(r_done, b)
                nc.scalar.copy(PT[:].rearrange("p t c -> p (t c)"), d_ps).then_inc(pt_ready, 1)

            def scale_r(b, par):
                act.wait_ge(rz_ready, b + 1)
                act.wait_ge(r_done, b + 1)
                if not isinstance(b, int) or b >= 2:
                    act.wait_ge(m_done, b - par)
                for t in range(NT):
                    nc.scalar.activation(R[:, t, par, :], r_ps[:, t * C:(t + 1) * C], ACT.Copy, scale=rz[:, t:t + 1]
                                         ).then_inc(r_ready, 1)

            def act_step(b, par):
                split_hi(b, 0)
                exp(b, 1)
                keep_pt(b - 1)
                split_hi(b, 1)
                exp(b + 1, 0)
                scale_r(b - 1, 1 - par)

            exp(0, 0)
            keep_xt(UNITS - 3)
            act.wait_ge(u_done, 1)
            nc.scalar.activation(u_all[:].rearrange("p h c -> p (h c)"), ps[:, 6, :], ACT.Copy, scale=SCALE
                                 ).then_inc(u_ready, 1)
            split_hi(0, 0)
            exp(0, 1)
            keep_xt(UNITS - 2)
            act.wait_ge(ct_done, 1)
            nc.scalar.copy(wc_flat[:].rearrange("p t c -> p (t c)"), xt_ps[1][:, 0:TAPS * C]).then_inc(ct_kept, 1)
            split_hi(0, 1)
            exp(1, 0)
            keep_xt(UNITS - 1)
            act_step(1, 1)
            with act.Fori(2, LAST - 1, 2) as b:
                act_step(b, 0)
                act_step(b + 1, 1)
            act_step(LAST - 1, 0)

            def signs(q, d):
                act.wait_ge(sg_zeroed, 2)
                act.wait_ge(x1_ready, q + 1)
                half = slice(d * C, d * C + C)
                nc.scalar.activation(SG[half, 2 * q + d, 1:H + 1, 1:W + 1],
                                     X[half, q, :].rearrange("p (h w) -> p h w", h=H), ACT.Sign
                                     ).then_inc(sg_ready, 1)

            def keep_y(h):
                act.wait_ge(conv_done, h + 1)
                nc.scalar.copy(Y[:, h * BANK:(h + 1) * BANK], c_ps[0][:, h * BANK:(h + 1) * BANK]).then_inc(y_ready, 1)

            split_hi(LAST, 0)
            exp(LAST, 1)
            keep_pt(LAST - 1)
            split_hi(LAST, 1)
            for d in two:
                signs(0, d)
            scale_r(LAST - 1, 0)
            keep_pt(LAST)
            signs(1, 0)
            scale_r(LAST, 1)
            signs(1, 1)
            for d in two:
                signs(2, d)
            keep_y(0)
            keep_y(1)
            for d in two:
                signs(3, d)

            act.wait_ge(fold_done, 1)
            nc.scalar.activation(bn[:, BN_SPREAD], fs_ps[:, 2:3], ACT.Square).then_inc(bn_act, 1)
            act.wait_ge(bn_act, 1)
            nc.scalar.activation(bn[:, BN_LN], fs_ps[:, 1:2], ACT.Ln, bias=bn[:, BN_SPREAD]).then_inc(bn_act, 1)
            act.wait_ge(bn_act, 2)
            nc.scalar.activation(bn[:, BN_INV], bn[:, BN_LN], ACT.Exp, scale=-0.5).then_inc(bn_act, 1)
            act.wait_ge(affine_ready, 1)
            for q, part in OUT_PARTS:
                src = Y[:, part] if q == 0 else c_ps[q][:, part]
                nc.scalar.activation(XN[:, q, part], src, ACT.Identity, bias=bn[:, BN_SHIFT], scale=bn[:, BN_SCALE]
                                     ).then_inc(t_ready, 1)

        @block.vector
        def _(dve):
            nc.vector.memset(mean_mat[:], 0.0).then_inc(mats_ready, 1)
            nc.vector.memset(eps[:], LN_EPS).then_inc(dve_const, 1)
            dve.wait_ge(mats_ready, 1)
            for d in two:
                nc.vector.memset(mean_mat[d * C:d * C + C, d * C:d * C + C], 1.0 / C).then_inc(mats_ready, 1)
            dve.wait_ge(ident_ready, 1)
            dve.wait_ge(mats_ready, 3)
            nc.vector.tensor_tensor(center_mat[:], ident[:], mean_mat[:], ALU.subtract).then_inc(mats_ready, 1)
            nc.vector.tensor_copy(ident_bf[:], ident[:]).then_inc(dve_const, 1)
            nc.vector.tensor_tensor(unfold[:, 0:C], ident[:, 0:C], ident[:, C:P], ALU.add).then_inc(dve_const, 1)
            dve.wait_ge(dve_const, 3)
            for d in two:
                nc.vector.tensor_scalar(fold[:, d, :], unfold[:, 0:C], 0.5, None, ALU.mult).then_inc(dve_const, 1)
                nc.vector.tensor_scalar(fold_neg[:, d, :], unfold[:, 0:C], -0.5, None, ALU.mult).then_inc(dve_const, 1)
            dve.wait_ge(dve_const, 7)
            nc.vector.tensor_tensor(unfold[:], ident[:], fold[:].rearrange("p d c -> p (d c)"),
                                    ALU.subtract).then_inc(dve_const, 1)
            nc.vector.memset(wo_heads[:], 0.0).then_inc(heads_zeroed, 1)
            nc.vector.memset(wc_t[:], 0.0).then_inc(wct_zeroed, 1)
            def normalise(n):
                q, h = n // HALVES, n % HALVES
                part = slice(h * BANK, (h + 1) * BANK)
                dve.wait_ge(rstd_ready, n + 1)
                nc.vector.scalar_tensor_tensor(XN[:, q, part], pc[n % 4], vec[:, G_:G_ + 1], rstd[:, n % 2, :],
                                               op0=ALU.mult, op1=ALU.mult).then_inc(scaled, 1)

            def split_x(n):
                q, h = n // HALVES, n % HALVES
                part = slice(h * BANK, (h + 1) * BANK)
                dve.wait_ge(scaled, n + 1)
                if n >= 4:
                    dve.wait_ge(xt_done, n - 3)
                    dve.wait_ge(stacked[q - 2], 64)
                nc.vector.tensor_scalar(x_hi[:, q % 2, part], XN[:, q, part], vec[:, B_:B_ + 1], None, ALU.add
                                        ).then_inc(hi_ready, 1)
                dve.wait_ge(hi_ready, n + 1)
                nc.vector.scalar_tensor_tensor(x_lo[:, q % 2, part], XN[:, q, part], vec[:, B_:B_ + 1],
                                               x_hi[:, q % 2, part], op0=ALU.add, op1=ALU.subtract
                                               ).then_inc(lo_ready, 1)

            def keep_xt(n):
                q, h = n // HALVES, n % HALVES
                dve.wait_ge(xt_done, n + 1)
                nc.vector.tensor_copy(XT[:, 2 * q:2 * q + 2, h * CPB:(h + 1) * CPB]
                                      .rearrange("p b k e c -> p (k e) b c"),
                                      xt_ps[n % 2].rearrange("p (k b c) -> p k b c", b=2, c=C)
                                      ).then_inc(xt_kept[n % 2], 1)

            def row_max(b, t):
                dve.wait_ge(k_ready[t], b + 1)
                nc.vector.tensor_reduce(negmax[:, t:t + 1], k_ps[t], AX.X, ALU.max, negate=True
                                        ).then_inc(max_ready[t], 1)

            dve.wait_ge(wkt_done, 1)
            nc.vector.tensor_copy(vec[:, 0:5], ps[:, 6, NT * P:NT * P + 5]).then_inc(vec_ready, 1)
            nc.vector.tensor_copy(wk_hi[:].rearrange("p t c -> p (t c)"), ps[:, 6, 0:NT * P]).then_inc(wkh_ready, 1)
            dve.wait_ge(wkh_ready, 1)
            nc.vector.tensor_tensor(wk_lo[:].rearrange("p t c -> p (t c)"), ps[:, 6, 0:NT * P],
                                    wk_hi[:].rearrange("p t c -> p (t c)"), ALU.subtract).then_inc(wkl_ready, 1)
            dve.wait_ge(vec_ready, 1)
            nc.vector.tensor_tensor(vec[:, BS_:BS_ + 1], vec[:, B_:B_ + 1], vec[:, BO_:BO_ + 1], ALU.add
                                    ).then_inc(vec_ready, 1)
            for n in range(UNITS - 2):
                normalise(n)
                split_x(n)
                if n - 2 in XT_BY_DVE:
                    keep_xt(n - 2)
            row_max(0, 0)
            for n in (UNITS - 2, UNITS - 1):
                normalise(n)
            split_x(UNITS - 2)

            def split_lo(b, t):
                for h in two:
                    dve.wait_ge(eth_ready[h], b * 2 + t + 1)
                    dve.wait_ge(d_done[t], b)
                    nc.vector.tensor_tensor(et_lo[:, t, h * BANK:(h + 1) * BANK], t_ps[h],
                                            et_hi[:, t, h * BANK:(h + 1) * BANK], ALU.subtract
                                            ).then_inc(etl_ready[h], 1)

            def reciprocal_z(b):
                dve.wait_ge(exp_ready[1], b + 1)
                dve.wait_ge(exp_ready[0], b + 1)
                if not isinstance(b, int) or b:
                    dve.wait_ge(r_ready, b * 2)
                nc.vector.reciprocal(rz[:], Z[:, bass.ds(b, 1), :].rearrange("p b t -> p (b t)")).then_inc(rz_ready, 1)

            def split_m(b):
                dve.wait_ge(m_done, b + 2)
                hi, lo = (MM[:, bass.ds(b, 2), e, :] for e in two)
                m = m_ps.rearrange("p (b c) -> p b c", c=C)
                nc.vector.tensor_scalar(hi, m, 1.0, None, ALU.mult).then_inc(mm_ready, 2)
                dve.wait_ge(mm_ready, b * 2 + 2)
                nc.vector.tensor_tensor(lo, m, hi, ALU.subtract).then_inc(mm_ready, 2)

            def dve_step(b, pair_ready):
                row_max(b, 1)
                if pair_ready:
                    split_m(b - 3)
                split_lo(b, 0)
                row_max(b + 1, 0)
                reciprocal_z(b - 1)
                split_lo(b, 1)

            row_max(0, 1)
            split_lo(0, 0)
            row_max(1, 0)
            split_x(UNITS - 1)
            split_lo(0, 1)
            dve_step(1, False)
            with dve.Fori(2, LAST - 1, 2) as b:
                dve_step(b, False)
                dve_step(b + 1, True)
            dve_step(LAST - 1, False)
            def add_input(q):
                dve.wait_ge(f_done[q % 2], q // 2 + 1)
                nc.vector.scalar_tensor_tensor(X[:, q, :], f_ps[q % 2], vec[:, BS_:BS_ + 1], XN[:, q, :],
                                               op0=ALU.add, op1=ALU.add).then_inc(x1_ready, 1)

            def statistics(q, h):
                part = slice(h * BANK, (h + 1) * BANK)
                if q == 0:
                    dve.wait_ge(y_ready, h + 1)
                else:
                    dve.wait_ge(conv_done, HALVES * q + h + 1)
                nc.vector.bn_stats(ST[:, q, h, :], Y[:, part] if q == 0 else c_ps[q][:, part]).then_inc(st_ready, 1)

            row_max(LAST, 1)
            split_m(LAST - 3)
            reciprocal_z(LAST - 1)
            split_lo(LAST, 0)
            add_input(0)
            split_lo(LAST, 1)
            add_input(1)
            reciprocal_z(LAST)
            add_input(2)
            split_m(LAST - 1)
            add_input(3)
            for q in range(PAIRS):
                for h in range(HALVES):
                    statistics(q, h)

            dve.wait_ge(st_ready, PAIRS * HALVES)
            nc.vector.bn_aggr(MV[:], ST[:].rearrange("p q h e -> p (q h e)")).then_inc(mv_ready, 1)
            dve.wait_ge(bn_act, 3)
            nc.vector.tensor_tensor(bn[:, BN_SCALE], bn[:, BN_INV], vec[:, GA_:GA_ + 1], ALU.mult
                                    ).then_inc(scale_ready, 1)
            dve.wait_ge(scale_ready, 1)
            nc.vector.scalar_tensor_tensor(bn[:, BN_SHIFT], fs_ps[:, 0:1], bn[:, BN_SCALE], vec[:, BE_:BE_ + 1],
                                           op0=ALU.mult, op1=ALU.add).then_inc(affine_ready, 1)
            for n, (q, part) in enumerate(OUT_PARTS):
                if n not in POOL_PARTS:
                    dve.wait_ge(t_ready, n + 1)
                    nc.vector.tensor_tensor(XN[:, q, part], XN[:, q, part], X[:, q, part], ALU.add
                                            ).then_inc(o_dve, 1)

        @block.tensor
        def _(pe):
            def center(n):
                q, h = n // HALVES, n % HALVES
                pe.wait_ge(x_loaded[n if q == 0 else q + 1], 16)
                if n >= 4:
                    pe.wait_ge(scaled, n - 3)
                nc.tensor.matmul(pc[n % 4], center_mat[:], X[:, q, h * BANK:(h + 1) * BANK], start=True, stop=True
                                 ).then_inc(centered, 1)

            def variance(n):
                pe.wait_ge(squared, n + 1)
                if n >= 2:
                    pe.wait_ge(lnv_ready, n - 1)
                nc.tensor.matmul(pv[n % 2], mean_mat[:], sq[:, n % 2, :], start=True, stop=True
                                 ).then_inc(var_done, 1)

            def transpose_x(n):
                q, h = n // HALVES, n % HALVES
                pe.wait_ge(lo_ready, n + 1)
                if n >= 2:
                    pe.wait_ge(xt_kept[n % 2], n // 2)
                for k in range(CPB):
                    for e, src in enumerate((x_hi, x_lo)):
                        last = nc.tensor.transpose(xt_ps[n % 2][:, (2 * k + e) * P:(2 * k + e + 1) * P],
                                                   src[:, q % 2, (h * CPB + k) * P:(h * CPB + k + 1) * P],
                                                   ident_bf[:])
                last.then_inc(xt_done, 1)

            def keys(b, t):
                pe.wait_ge(exp_ready[t], b)
                for w, first in ((wk_hi, True), (wk_lo, False)):
                    for h in two:
                        last = nc.tensor.matmul(k_ps[t][:, h * BANK:(h + 1) * BANK], w[:, t, :],
                                                S[:, bass.ds(b, 1), h * BANK:(h + 1) * BANK]
                                                .rearrange("p b n -> p (b n)"), start=first, stop=not first)
                last.then_inc(k_ready[t], 1)

            pe.wait_ge(mats_ready, 3)
            for _ in range(WARM):
                nc.tensor.matmul(ps[:, 7, 0:P], mean_mat[:], mean_mat[:], start=True, stop=True)
            pe.wait_ge(mats_ready, 4)
            center(0)
            center(1)
            pe.wait_ge(wo_loaded, 16)
            for t in range(NT):
                last = nc.tensor.transpose(ps[:, 7, t * C:(t + 1) * C], wo_in[:, t * P:(t + 1) * P], ident[0:C, 0:C])
            last.then_inc(wot_done, 1)
            variance(0)
            pe.wait_ge(vec_loaded, 5 * 16)
            nc.tensor.transpose(ps[:, 6, NT * P:NT * P + 5], vec_rows[:].rearrange("v d c -> v (d c)"),
                                ident[0:5, 0:5])
            pe.wait_ge(wk_loaded, 32)
            for t in range(NT):
                last = nc.tensor.transpose(ps[:, 6, t * P:(t + 1) * P], wk_in[:, t].rearrange("p d i -> p (d i)"),
                                           ident[:])
            last.then_inc(wkt_done, 1)
            variance(1)
            center(2)
            center(3)
            for n in range(2, UNITS):
                variance(n)
                if n + 2 < UNITS:
                    center(n + 2)
                if n == 2:
                    pe.wait_ge(wkl_ready, 1)
                if n == 3:
                    pe.wait_ge(heads_ready, HPT)
                if n == UNITS - 1:
                    pe.wait_ge(wkl_ready, 1)
                    pe.wait_ge(stacked[0], 64)
                    pe.wait_ge(scaled, UNITS - 2)
                    keys(0, 0)
                transpose_x(n - 2)

            def transpose_e(b, t):
                pe.wait_ge(exp_ready[t], b + 1)
                for h in two:
                    pe.wait_ge(etl_ready[h], b * 2 + t)
                    for k in range(CPB):
                        last = nc.tensor.transpose(t_ps[h][:, k * P:(k + 1) * P],
                                                   E[:, t, (h * CPB + k) * P:(h * CPB + k + 1) * P], ident[:])
                    last.then_inc(et_done[h], 1)

            def context(b, t, par=0):
                if t == 0:
                    pe.wait_ge(pt_ready, b)
                xt = XT[:, b] if isinstance(b, int) else XT_ring[:, par]
                for h in two:
                    pe.wait_ge(etl_ready[h], b * 2 + t + 1)
                    for k in range(h * CPB, (h + 1) * CPB):
                        nc.tensor.matmul(d_ps[:, t * P:(t + 1) * P], xt[:, k].rearrange("p d c -> p (d c)"),
                                         et_hi[:, t, k * P:(k + 1) * P], start=(k == 0), stop=False)
                    for k in range(h * CPB, (h + 1) * CPB):
                        d = k % 2
                        last = nc.tensor.matmul(d_ps[d * C:d * C + C, t * P:(t + 1) * P], xt[:, k, 0, :],
                                                et_lo[:, t, k * P:(k + 1) * P], start=False, stop=(k >= CH - 2))
                last.then_inc(d_done[t], 1)

            def project(b, par):
                pe.wait_ge(pt_ready, b + 1)
                if not isinstance(b, int) or b:
                    pe.wait_ge(r_ready, b * 2)
                else:
                    pe.wait_ge(xt_kept[1], UNITS // 2)
                if not isinstance(b, int) or b >= 2:
                    pe.wait_ge(mm_ready, (b - par) * 2)
                for h in range(HEADS):
                    t, g = h // HPT, h % HPT
                    last = nc.tensor.matmul(r_ps[g * DH:(g + 1) * DH, t * C:(t + 1) * C],
                                            PT[:, t, g * DH:(g + 1) * DH], u_all[:, h, :], start=True, stop=True)
                last.then_inc(r_done, 1)

            def matrix(b):
                pe.wait_ge(r_ready, b * 2 + 4)
                for t in range(NT):
                    last = nc.tensor.matmul(m_ps, wq_in[:, t].rearrange("p d i -> p (d i)"),
                                            R[:, t].rearrange("p b c -> p (b c)"), start=(t == 0),
                                            stop=(t == NT - 1))
                last.then_inc(m_done, 2)

            def pe_step(b, par, pair_ready):
                transpose_e(b, 0)
                if pair_ready:
                    matrix(b - 3)
                context(b - 1, 1, 1 - par)
                keys(b + 1, 0)
                transpose_e(b, 1)
                project(b - 1, 1 - par)
                if not isinstance(b, int):
                    pe.wait_ge(ring_ready[par], (b + par) * 8)
                context(b, 0, par)
                keys(b + 1, 1)

            pe.wait_ge(xt_kept[0], UNITS // 2 - 1)
            pe.wait_ge(wv_loaded, 32)
            for t in range(NT):
                last = nc.tensor.matmul(ps[:, 6, t * HPT * C:(t + 1) * HPT * C],
                                        wv_in[:, t].rearrange("p d i -> p (d i)"),
                                        wo_heads[:, t].rearrange("p h c -> p (h c)"), start=True, stop=True)
            last.then_inc(u_done, 1)
            pe.wait_ge(scaled, UNITS)
            keys(0, 1)
            pe.wait_ge(lnv_ready, UNITS)
            transpose_e(0, 0)
            pe.wait_ge(u_ready, 1)
            transpose_x(UNITS - 2)
            pe.wait_ge(wsign_ready, 2)
            pe.wait_ge(xt_kept[1], UNITS // 2 - 1)
            for k in range(TAPS):
                last = nc.tensor.transpose(xt_ps[1][:, k * C:(k + 1) * C],
                                           wc_sign[:, k].rearrange("o d i -> o (d i)"), ident_bf[0:C, 0:C])
            last.then_inc(ct_done, 1)
            keys(1, 0)
            transpose_e(0, 1)
            pe.wait_ge(xt_kept[0], UNITS // 2)
            context(0, 0)
            pe.wait_ge(ct_kept, 1)
            transpose_x(UNITS - 1)
            keys(1, 1)
            pe.wait_ge(wq_loaded, 32)
            pe.wait_ge(stacked[1], 64)
            pe_step(1, 1, False)
            for q in range(2, PAIRS):
                pe.wait_ge(stacked[q], 64)
            pe.wait_ge(ring_ready[1], 16)
            with pe.Fori(2, LAST - 1, 2) as b:
                pe_step(b, 0, False)
                pe_step(b + 1, 1, True)
            pe_step(LAST - 1, 0, False)
            def apply_matrix(q):
                pe.wait_ge(mm_ready, 4 * q + 4)
                pe.wait_ge(x1_ready, max(q - 1, 0))
                for h in range(HALVES):
                    for e in two:
                        for d in two:
                            last = nc.tensor.matmul(f_ps[q % 2][d * C:d * C + C, h * BANK:(h + 1) * BANK],
                                                    MM[:, 2 * q + d, e, :],
                                                    S[:, 2 * q + d, h * BANK:(h + 1) * BANK],
                                                    start=(e == 0), stop=(e == 1))
                last.then_inc(f_done[q % 2], 1)

            def convolve(q, h):
                pe.wait_ge(shifted[q], 32)
                pe.wait_ge(sg_ready, 2 * q + 2)
                if q >= 2:
                    pe.wait_ge(x1_ready, q + 1)
                for k in range(6):
                    r, c = h * ROWS + k // 3, k % 3
                    for d in two:
                        last = nc.tensor.matmul(c_ps[q][d * C:d * C + C, h * BANK:(h + 1) * BANK],
                                                wc_t[:, d, k, :], SG[:, 2 * q + d, r:r + ROWS, c:c + W],
                                                start=(k == 0), stop=(k == 5))
                last.then_inc(conv_done, 1)

            pe.wait_ge(wct_ready, 6)
            transpose_e(LAST, 0)
            matrix(LAST - 3)
            apply_matrix(0)
            context(LAST - 1, 1)
            transpose_e(LAST, 1)
            apply_matrix(1)
            project(LAST - 1, 0)
            context(LAST, 0)
            context(LAST, 1)
            apply_matrix(2)
            for h in two:
                pe.wait_ge(etl_ready[h], B * NT)
            project(LAST, 1)
            matrix(LAST - 1)
            convolve(0, 0)
            apply_matrix(3)
            convolve(0, 1)
            pe.wait_ge(pt_ready, B)
            pe.wait_ge(mm_ready, 2 * B)
            for q in range(1, PAIRS):
                for h in range(HALVES):
                    convolve(q, h)

            fold_mat, fold_neg_mat = fold[:].rearrange("p d c -> p (d c)"), fold_neg[:].rearrange("p d c -> p (d c)")
            pe.wait_ge(y_ready, HALVES)
            nc.tensor.matmul(fs_ps[:, 1:2], fold_mat, eps[:], start=True, stop=False)
            pe.wait_ge(mv_ready, 1)
            nc.tensor.matmul(fs_ps[:, 1:2], fold_mat, MV[:, 1:2], start=False, stop=True)
            nc.tensor.matmul(fs_ps[:, 0:1], fold_neg_mat, MV[:, 0:1], start=True, stop=True)
            nc.tensor.matmul(fs_ps[:, 2:3], unfold[:], MV[:, 0:1], start=True, stop=True).then_inc(fold_done, 1)


_INS = ["x", "L0_conv_g", "L0_conv_b", "L0_conv_w_qkv", "L0_conv_w_out", "L0_conv_b_out", "L1_conv_W",
        "L1_conv_gamma", "L1_conv_beta"]


def kernel(**inputs):
    import numpy as _np
    import concourse.bacc as _bacc
    from concourse import mybir as _mybir
    from concourse.bass_utils import run_bass_kernel_spmd as _run

    nc = _bacc.Bacc("TRN2", target_bir_lowering=False, num_devices=1)
    arrays, args = {}, []
    for name in _INS:
        a = _np.ascontiguousarray(inputs[name])
        arrays[f"in_{name}"] = a
        args.append(nc.dram_tensor(f"in_{name}", a.shape, _mybir.dt.from_np(a.dtype), kind="ExternalInput").ap())
    shape = _np.shape(inputs["x"])
    out = nc.dram_tensor("out_0", shape, _mybir.dt.float32, kind="ExternalOutput").ap()
    attention_then_binary_conv(nc, *args, out)
    r = _run(nc, [arrays], core_ids=[0])
    return r.results[0]["out_0"]
```
